# Optimizing a Trainium2 kernel written in Bass

```python
import numpy as np
import jax
import jax.numpy as jnp

def _softmax(x, axis=-1):
    return jax.nn.softmax(x, axis=axis)

def _gelu(x):
    return jax.nn.gelu(x, approximate=True)

def _silu(x):
    return jax.nn.silu(x)

def _sigmoid(x):
    return jax.nn.sigmoid(x)

def _layernorm(x, axis=-1, eps=1e-05):
    m = jnp.mean(x, axis=axis, keepdims=True)
    v = jnp.var(x, axis=axis, keepdims=True)
    return (x - m) / jnp.sqrt(v + eps)

def _scatter_add(tgt, idx, src, axis=0):
    return tgt.at[idx].add(src)

def _segment_sum(src, seg, n):
    return jax.ops.segment_sum(src, seg, n)
kernel_name = 'mk_flamingo_gated_d1_seqx_r4_f1c723'

def setup_inputs(seed: int=0):
    np.random.seed(seed)
    _w = jnp.asarray

    def _rec_inputs():
        import jax
        import jax.numpy as jnp
        _rk = jax.random.key(seed)
        x = 7.22e-05 + 1 * jax.random.normal(jax.random.fold_in(_rk, 1), (4, 512, 512), jnp.float32)
        _lenS = 512 - jax.random.randint(jax.random.fold_in(_rk, 7), (4,), 0, max(1, 512 // 4) + 1, jnp.int32)
        _lenS2 = 512 - jax.random.randint(jax.random.fold_in(_rk, 8), (4,), 0, max(1, 512 // 4) + 1, jnp.int32)
        _ctx_1024P = jax.random.normal(jax.random.fold_in(_rk, 11), (4, 16, 256), jnp.float32)
        _ctx_1024c = jax.random.dirichlet(jax.random.fold_in(_rk, 511), 0.3 * jnp.ones((16,), jnp.float32), (4, 512))
        _ctx_1024t = jnp.einsum('bsk,bkd->bsd', _ctx_1024c, _ctx_1024P)
        _ctx_1024t = _ctx_1024t * jax.lax.rsqrt(jnp.mean(jnp.square(_ctx_1024t)) + 1e-12) * 0.953939
        ctx_1024 = 2.81802e-05 + 1.00001 * (_ctx_1024t + 0.3 * jax.random.normal(jax.random.fold_in(_rk, 611), (4, 512, 256), jnp.float32))
        _g = jax.random.normal(jax.random.fold_in(_rk, 9001), (2, 1), jnp.float32)
        _g = jnp.sign(_g) * jnp.maximum(jnp.abs(_g), 1.0) + (_g == 0) * 1.0
        g_xattn = _g[0]
        g_ffn = _g[1]
        return (x, ctx_1024, g_xattn, g_ffn)
    x, ctx_1024, g_xattn, g_ffn = _rec_inputs()

    def _L0_xattn_setup():
        import jax, jax.numpy as jnp
        import numpy as np
        key = jax.random.key(seed)
        ks = jax.random.split(key, 6)
        B, L, N, C, D = (8, 128, 512, 256, 128)
        return {'teacher_logits': jax.random.normal(ks[0], (B, L, N), dtype=jnp.float32), 'teacher_features': jax.random.normal(ks[1], (B, N, C), dtype=jnp.float32), 'Wq': jax.random.normal(ks[2], (D, C), dtype=jnp.float32) * (1.0 / np.sqrt(C)), 'bq': jnp.zeros((D,), dtype=jnp.float32), 'Wk': jax.random.normal(ks[3], (D, C), dtype=jnp.float32) * (1.0 / np.sqrt(C)), 'bk': jnp.zeros((D,), dtype=jnp.float32)}
    _L0_xattn_all = _L0_xattn_setup()
    _L0_xattn_in = {k: v for k, v in _L0_xattn_all.items() if k in ('Wq', 'bq', 'Wk', 'bk')}
    del _L0_xattn_all

    def _L0_ffn_setup():
        import jax, jax.numpy as jnp
        import numpy as np
        H = 512
        F = 352
        E = 64
        TOP_K = 6
        CAP = 128
        SCALE = 1.0
        F_SH = 2 * F
        B, S = (1, 512)
        key = jax.random.key(seed)
        ks = jax.random.split(key, 8)
        s = 0.02
        return {'hidden_states': jax.random.normal(ks[0], (B, S, H), jnp.float32), 'gate_w': jax.random.normal(ks[1], (E, H), jnp.float32) * s, 'w_gate': jax.random.normal(ks[2], (E, H, F), jnp.float32) * s, 'w_up': jax.random.normal(ks[3], (E, H, F), jnp.float32) * s, 'w_down': jax.random.normal(ks[4], (E, F, H), jnp.float32) * s, 'sh_gate': jax.random.normal(ks[5], (F_SH, H), jnp.float32) * s, 'sh_up': jax.random.normal(ks[6], (F_SH, H), jnp.float32) * s, 'sh_down': jax.random.normal(ks[7], (H, F_SH), jnp.float32) * s}
    _L0_ffn_all = _L0_ffn_setup()
    _L0_ffn_in = {k: v for k, v in _L0_ffn_all.items() if k in ('gate_w', 'w_gate', 'w_up', 'w_down', 'sh_gate', 'sh_up', 'sh_down')}
    del _L0_ffn_all
    return {'x': x, 'ctx_1024': ctx_1024, 'g_xattn': g_xattn, 'g_ffn': g_ffn, 'L0_xattn_Wq': _L0_xattn_in['Wq'], 'L0_xattn_bq': _L0_xattn_in['bq'], 'L0_xattn_Wk': _L0_xattn_in['Wk'], 'L0_xattn_bk': _L0_xattn_in['bk'], 'L0_ffn_gate_w': _L0_ffn_in['gate_w'], 'L0_ffn_w_gate': _L0_ffn_in['w_gate'], 'L0_ffn_w_up': _L0_ffn_in['w_up'], 'L0_ffn_w_down': _L0_ffn_in['w_down'], 'L0_ffn_sh_gate': _L0_ffn_in['sh_gate'], 'L0_ffn_sh_up': _L0_ffn_in['sh_up'], 'L0_ffn_sh_down': _L0_ffn_in['sh_down']}

def reference(x, ctx_1024, g_xattn, g_ffn, L0_xattn_Wq, L0_xattn_bq, L0_xattn_Wk, L0_xattn_bk, L0_ffn_gate_w, L0_ffn_w_gate, L0_ffn_w_up, L0_ffn_w_down, L0_ffn_sh_gate, L0_ffn_sh_up, L0_ffn_sh_down):
    import jax
    import jax.numpy as jnp

    def _L0_xattn_ref(teacher_logits, teacher_features, Wq, bq, Wk, bk):
        import jax, jax.numpy as jnp
        import numpy as np
        query = jnp.einsum('bnc,dc->bnd', teacher_features, Wq) + bq
        key = jnp.einsum('bnc,dc->bnd', teacher_features, Wk) + bk
        energy = jnp.einsum('bnd,bmd->bnm', query, key)
        attention = jax.nn.softmax(energy, axis=-1)
        x_m = jnp.einsum('bln,bmn->blm', teacher_logits, attention)
        return x_m

    def _L0_ffn_ref(hidden_states, gate_w, w_gate, w_up, w_down, sh_gate, sh_up, sh_down):
        import jax, jax.numpy as jnp
        import numpy as np
        H = 512
        F = 352
        E = 64
        TOP_K = 6
        CAP = 128
        SCALE = 1.0
        F_SH = 2 * F
        B, S = (1, 512)
        b, s, _ = hidden_states.shape
        x = hidden_states.reshape(-1, H)
        T = x.shape[0]
        logits = x.astype(jnp.float32) @ gate_w.astype(jnp.float32).T
        scores = jax.nn.softmax(logits, axis=-1)
        topk_w, topk_idx = jax.lax.top_k(scores, TOP_K)
        topk_w = topk_w * SCALE
        eid = topk_idx.reshape(-1)
        x_exp = jnp.repeat(x, TOP_K, axis=0)
        order = jnp.argsort(eid)
        eid_s = eid[order]
        counts = jnp.bincount(eid, length=E)
        starts = jnp.cumsum(counts) - counts
        pos = jnp.arange(T * TOP_K) - starts[eid_s]
        valid = pos < CAP
        pos_c = jnp.where(valid, pos, CAP)
        buf = jnp.zeros((E, CAP + 1, H), x.dtype).at[eid_s, pos_c].set(x_exp[order])
        g = jax.nn.silu(jnp.einsum('ech,ehf->ecf', buf, w_gate))
        u = jnp.einsum('ech,ehf->ecf', buf, w_up)
        d = jnp.einsum('ecf,efh->ech', g * u, w_down)
        out_s = jnp.where(valid[:, None], d[eid_s, pos_c], 0.0)
        out_exp = jnp.zeros_like(out_s).at[order].set(out_s)
        y = jnp.einsum('tkh,tk->th', out_exp.reshape(T, TOP_K, H), topk_w)
        y = y.astype(x.dtype).reshape(b, s, H)
        gs = jax.nn.silu(hidden_states @ sh_gate.T)
        us = hidden_states @ sh_up.T
        y = y + gs * us @ sh_down.T
        return y
    x = x + jnp.tanh(g_xattn[0]) * _L0_xattn_ref(_layernorm(x, axis=-1), ctx_1024, L0_xattn_Wq, L0_xattn_bq, L0_xattn_Wk, L0_xattn_bk)
    x = x + jnp.tanh(g_ffn[0]) * _L0_ffn_ref(_layernorm(x, axis=-1), L0_ffn_gate_w, L0_ffn_w_gate, L0_ffn_w_up, L0_ffn_w_down, L0_ffn_sh_gate, L0_ffn_sh_up, L0_ffn_sh_down)
    return x

_drawn_inputs = setup_inputs


def setup_inputs(seed=0):
    import zlib

    import numpy as np

    out = dict(_drawn_inputs(seed))
    spreads = {'L0_xattn_bq': (0.0, 0.1), 'L0_xattn_bk': (0.0, 2.0)}
    factors = {'L0_ffn_gate_w': 8.0,
     'L0_ffn_w_gate': 8.0,
     'L0_ffn_w_up': 8.0,
     'L0_ffn_w_down': 8.0,
     'L0_ffn_sh_gate': 8.0,
     'L0_ffn_sh_up': 8.0,
     'L0_ffn_sh_down': 8.0}
    for name, (base, spread) in spreads.items():
        noise = np.random.default_rng([zlib.crc32(name.encode()), seed]).standard_normal(out[name].shape)
        drawn = base * np.exp(spread * noise) if base else spread * noise
        out[name] = jnp.asarray(drawn.astype(out[name].dtype))
    for name, factor in factors.items():
        out[name] = (out[name] * factor).astype(out[name].dtype)
    return out
```

```python
import concourse.bass as bass
from concourse import mybir
from contextlib import ExitStack

P = 128
B, L, H, C, D = 4, 512, 512, 256, 128
T = B * L
E, F, TOPK, CAP = 64, 352, 6, 128
NT = T // P
NTB = L // P
FSH = 2 * F
ROW = H + E
GU = 4 * F
WALL = 2 * GU + 3 * H
ROWS = T + P
EPS = 1e-5

FP = mybir.dt.float32
FR = mybir.dt.float32r
I32 = mybir.dt.int32
ALU = mybir.AluOpType
ACT = mybir.ActivationFunctionType
AX = mybir.AxisListType
FOUND = -2.0e38
ABSENT = 3.0e38

FKS = [128, 128, F - 256]


def plan_jobs():
    jobs = []
    lead = 7
    tiles = list(range(NT))
    for t in tiles[:lead]:
        jobs += [("s", t, 0), ("s", t, 1)]
    rest = tiles[lead:]
    for e in range(E):
        jobs.append(("e", e))
        if rest and e % 7 == 3:
            t = rest.pop(0)
            jobs += [("s", t, 0), ("s", t, 1)]
    assert not rest
    return jobs, 2 * lead


class Queue:

    def __init__(self, book):
        self.book, self.steps, self.seen = book, [], {}

    def wait(self, *toks):
        for tok in toks:
            if tok is None:
                continue
            name, val = tok
            if self.seen.get(name, 0) < val:
                self.seen[name] = val
                sem = self.book.sem(name)
                self.steps.append(lambda eng, s=sem, v=val: eng.wait_ge(s, v))

    def do(self, fn, tag=None, by=1):
        if tag is None:
            self.steps.append(fn)
            return None
        tok = self.book.tick(tag, by)
        sem = self.book.sem(tag)
        self.steps.append(lambda eng: fn(eng).then_inc(sem, by))
        return tok

    def replay(self, eng):
        for s in self.steps:
            s(eng)


class Book:

    def __init__(self, nc, ctx):
        self.nc, self.ctx, self.sems, self.count = nc, ctx, {}, {}

    def sem(self, name):
        if name not in self.sems:
            self.sems[name] = self.ctx.enter_context(self.nc.semaphore(name))
        return self.sems[name]

    def tick(self, name, by):
        self.count[name] = self.count.get(name, 0) + by
        return (name, self.count[name])


def build(nc, x, ctxt, gx, gf, wq, bq, wk, bk, gw, wg, wu, wd, sg, su, sd, cst, y, rows):
    ctx = ExitStack()
    book = Book(nc, ctx)
    sp, act, pe, dve, pool = (Queue(book) for _ in range(5))

    def sb(stack, name, shape, dt=FP):
        return stack.enter_context(nc.sbuf_tensor(name, shape, dt))

    cs = sb(ctx, "cs", [P, 128 + 16 + 1])
    ident, ktab, pcol = cs[:, 0:128], cs[:, 128:144], cs[:, 144:145]
    SWH = [sb(ctx, f"SWH{s}", [P, WALL], FR) for s in range(2)]
    SWL = [sb(ctx, f"SWL{s}", [P, WALL], FR) for s in range(2)]
    RW = [sb(ctx, f"RW{s}", [P, WALL]) for s in range(2)]
    idx = sb(ctx, "idx", [P, E], I32)
    tg2 = sb(ctx, "tg2", [P, 4])
    tgx, tgf = tg2[:, 2:3], tg2[:, 3:4]
    tiny = sb(ctx, "tiny", [P, 64])

    PS = [ctx.enter_context(nc.psum_tensor(f"PS{i}", [P, 512], FP)) for i in range(8)]

    actx = ExitStack()
    xs = [sb(actx, f"xs{i}", [P, NTB, H]) for i in range(2)]
    cx = sb(actx, "cx", [P, 2, L])
    wqs = sb(actx, "wqs", [P, 2, D])
    wks = sb(actx, "wks", [P, 2, D])
    bqk = sb(actx, "bqk", [P, 2])
    gws = sb(actx, "gws", [P, 4, E])
    lnx = sb(actx, "lnx", [P, NTB, H])
    lTh = sb(actx, "lTh", [P, 4, L], FR)
    lTl = sb(actx, "lTl", [P, 4, L], FR)
    QT = sb(actx, "QT", [P, L])
    KT = sb(actx, "KT", [P, L])
    At = sb(actx, "At", [P, NTB, L])
    ATh = sb(actx, "ATh", [P, 4, L], FR)
    ATl = sb(actx, "ATl", [P, 4, L], FR)
    l2T = sb(actx, "l2T", [P, 4, P])
    r2 = sb(actx, "r2", [P, NTB, ROW])
    st = sb(actx, "st", [P, 2, NTB, 6])
    mv = sb(actx, "mv", [P, 2, NTB, 2])
    rs = sb(actx, "rs", [P, 2, 4, NTB])
    sm = sb(actx, "sm", [P, 8, NTB])
    v8 = sb(actx, "v8", [P, 2, 8])
    mr = sb(actx, "mr", [P, E])
    KM = sb(actx, "KM", [P, 8, 2 * E])
    keyT = sb(actx, "keyT", [P, 1024])
    LA = sb(actx, "LA", [P, P])
    L2 = sb(actx, "L2", [E, 2 * P])
    LF = sb(actx, "LF", [E, P])
    t12 = sb(actx, "t12", [P, 2, E])
    actx.close()

    WH, WL = [None, None], [None, None]
    WH[0], WL[0] = sb(ctx, "WH0", [P, WALL], FR), sb(ctx, "WL0", [P, WALL], FR)
    NXG = 3
    XG = [sb(ctx, f"XG{i}", [P, ROW]) for i in range(NXG)]
    xTh = [sb(ctx, f"xTh{i}", [P, 512], FR) for i in range(2)]
    xTl = [sb(ctx, f"xTl{i}", [P, 512], FR) for i in range(2)]
    sg_ = [sb(ctx, f"sgl{i}", [P, F]) for i in range(1)]
    hg = [sb(ctx, f"hg{i}", [P, F]) for i in range(1)]
    hTh = [sb(ctx, f"hTh{i}", [P, 384], FR) for i in range(1)]
    hTl = [sb(ctx, f"hTl{i}", [P, 384], FR) for i in range(1)]
    ob = [sb(ctx, f"ob{i}", [P, H]) for i in range(2)]
    WH[1], WL[1] = sb(ctx, "WH1", [P, WALL], FR), sb(ctx, "WL1", [P, WALL], FR)

    f32 = lambda ap: ap.bitcast(FP)
    dma = lambda q, out, in_, tag, **kw: q.do(lambda g: g.dma_start(out, in_, **kw), tag, 16)

    def load_x(b):
        sp.wait(x_free.get(b - 2), stored.get(b - 2))
        x_in[b] = dma(sp, xs[b % 2][:, :, :], x[b].rearrange("(i p) n -> p i n", p=P), f"in_x{b % 2}")

    def load_ctx(b):
        sp.wait(ctx_free.get(b - 1))
        c_in[b] = dma(sp, cx[:, :, :], ctxt[b].rearrange("(k p) n -> p k n", p=P), "in_ctx")

    x_in, c_in, x_free, ctx_free, stored = {}, {}, {}, {}, {}
    load_x(0)
    load_ctx(0)
    for o, i in ((wqs, wq), (wks, wk)):
        w_in = dma(sp, o[:, :, :], i.rearrange("(k p) d -> p k d", p=P), "in_w")
    w_in = dma(sp, bqk[:, 0:1], bq, "in_w")
    w_in = dma(sp, bqk[:, 1:2], bk, "in_w")
    cst_in = dma(act, cs[:, :], cst, "in_cst")
    g_in = dma(act, tg2[:, 0:1], gx.to_broadcast([P, 1]), "in_g")
    g_in = dma(act, tg2[:, 1:2], gf.to_broadcast([P, 1]), "in_g")
    gw_in = dma(act, gws[:, :, :], gw.rearrange("(p k) e -> p k e", k=4), "in_gw")
    load_x(1)
    raw_in, raw_free = {}, {}

    def unit(u):
        return slice({"G": 0, "U": GU, "D": 2 * GU}[u], {"G": GU, "U": 2 * GU, "D": WALL}[u])

    def load_raw(n, u):
        t = RW[n % 2]
        sp.wait(*raw_free.get((n - 2, u), ()))
        if n < 2:
            cols = slice(n * F, (n + 1) * F)
            g_, u_, d_ = sg[:, cols], su[:, cols], sd[n * F:(n + 1) * F, :]
        else:
            g_, u_, d_ = wg[n - 2], wu[n - 2], wd[n - 2]
        tag = f"raw{u}{n % 2}"
        if u in "GU":
            src = (g_ if u == "G" else u_).rearrange("(p k) f -> p k f", k=4)
            tok = dma(sp, t[:, unit(u)].rearrange("p (k f) -> p k f", k=4), src, tag)
        else:
            o = 2 * GU
            dma(sp, t[:, o:o + 2 * H].rearrange("p (k n) -> p k n", k=2),
                d_[0:256, :].rearrange("(k p) n -> p k n", p=P), tag)
            tok = dma(sp, t[0:FKS[2], o + 2 * H:o + 3 * H], d_[256:F, :], tag)
        raw_in[n, u] = tok

    for n in range(2):
        for u in "GUD":
            load_raw(n, u)

    set_ready, set_freed = {}, {}

    def pieces(u):
        if u in "GU":
            s = unit(u)
            return [(P, s.start, s.stop)]
        o = 2 * GU
        return [(P, o, o + 2 * H), (FKS[2], o + 2 * H, o + 3 * H)]

    def dest(n):
        return (SWH[n], SWL[n]) if n < 2 else (WH[n % 2], WL[n % 2])

    def split_high(q, n, u, what):
        h, _ = dest(n)
        q.wait(raw_in[n, u], *set_freed.get((n - 2, u), ()))
        for np_, a, b in pieces(u):
            if q is act:
                fn = lambda g, np_=np_, a=a, b=b: g.activation(h[0:np_, a:b], RW[n % 2][0:np_, a:b], ACT.Copy)
            else:
                fn = lambda g, np_=np_, a=a, b=b: g.tensor_copy(h[0:np_, a:b], RW[n % 2][0:np_, a:b])
            tok = q.do(fn, what)
        return tok

    def split_low(q, n, u, high, what):
        h, l = dest(n)
        q.wait(raw_in[n, u], *set_freed.get((n - 2, u), ()), high)
        for np_, a, b in pieces(u):
            tok = q.do(lambda g, np_=np_, a=a, b=b: g.tensor_tensor(
                l[0:np_, a:b], RW[n % 2][0:np_, a:b], f32(h[0:np_, a:b]), ALU.subtract), what)
        raw_free[n, u] = (tok,)
        set_ready[n, u] = (high, tok)

    for n in range(2):
        for u in "GUD":
            hi = split_high(pool, n, u, "pool_wh")
            split_low(pool, n, u, hi, "pool_wl")
    for e in range(2):
        for u in "GUD":
            load_raw(2 + e, u)

    act.wait(g_in)
    tg_ready = act.do(lambda g: g.activation(tg2[:, 2:4], tg2[:, 0:2], ACT.Tanh), "act_tg")
    vr = dve.do(lambda g: g.memset(v8[:, 1, :], ABSENT), "dve_vr")
    nh = pool.do(lambda g: g.memset(rs[:, 0, 3, :], -0.5), "pool_nh")
    nh = pool.do(lambda g: g.memset(rs[:, 1, 3, :], -0.5), "pool_nh")

    ps_free = [() for _ in range(8)]

    def norm_stats(w, src, src_toks, b):
        dve.wait(*src_toks)
        for i in range(NTB):
            s = dve.do(lambda g, i=i: g.bn_stats(st[:, w, i, :], src[:, i, :]), "dve_st")
        dve.wait(s)
        for i in range(NTB):
            s = dve.do(lambda g, i=i: g.bn_aggr(mv[:, w, i, :], st[:, w, i, :]), "dve_mv")
        pool.wait(s, nh)
        ve, r, t = (rs[:, w, k, :] for k in range(3))
        s = pool.do(lambda g: g.tensor_scalar(ve, mv[:, w, :, 1], EPS, None, ALU.add), "pool_rs")
        pool.wait(s)
        s = pool.do(lambda g: g.tensor_tensor(r, ve, rs[:, w, 3, :], ALU.pow), "pool_rs")
        pool.wait(s)
        s = pool.do(lambda g: g.tensor_tensor(t, r, r, ALU.mult), "pool_rs")
        pool.wait(s)
        s = pool.do(lambda g: g.tensor_tensor(t, t, ve, ALU.mult), "pool_rs")
        pool.wait(s)
        s = pool.do(lambda g: g.tensor_scalar(t, t, -0.5, 1.5, ALU.mult, ALU.add), "pool_rs")
        pool.wait(s)
        s = pool.do(lambda g: g.tensor_tensor(r, r, t, ALU.mult), "pool_rs")
        return s

    ln_free, ln_done, T_use = {}, {}, [0]

    def layer1(b):
        r = norm_stats(0, xs[b % 2], [x_in[b]], b)
        dve.wait(r, ln_free.get(b - 1))
        for i in range(NTB):
            s = dve.do(lambda g, i=i: g.tensor_scalar(lnx[:, i, :], xs[b % 2][:, i, :], mv[:, 0, i, 0:1],
                                                      rs[:, 0, 1, i:i + 1], ALU.subtract, ALU.mult), "dve_ln")
        ln_done[b] = s

    def t_bank():
        k = T_use[0] % 2
        T_use[0] += 1
        return k

    lT_ready, xm_done = {}, {}

    def transpose_ln(b):
        pe.wait(ln_done[b], cst_in)
        for i in range(NTB):
            k = t_bank()
            pe.wait(*ps_free[k])
            for c in range(4):
                fn = lambda g, i=i, c=c, k=k: g.transpose(PS[k][:, c * P:(c + 1) * P],
                                                          lnx[:, i, c * P:(c + 1) * P], ident)
                s = pe.do(fn, "pe_tx" if c == 3 else None)
            act.wait(s, xm_done.get(b - 1))
            dst = lambda t, i=i: t[:, :, i * P:(i + 1) * P]
            src = PS[k][:, :].rearrange("p (c m) -> p c m", c=4)
            hi = act.do(lambda g, i=i, src=src: g.activation(dst(lTh), src, ACT.Copy), "act_lT") if False else \
                act.do(lambda g, i=i, src=src: g.activation(lTh[:, :, i * P:(i + 1) * P], src, ACT.Copy), "act_lT")
            dve.wait(s, hi, xm_done.get(b - 1))
            lo = dve.do(lambda g, i=i, src=src: g.tensor_tensor(
                lTl[:, :, i * P:(i + 1) * P], src, f32(lTh[:, :, i * P:(i + 1) * P]), ALU.subtract), "dve_lT")
            ps_free[k] = (hi, lo)
        ln_free[b] = s
        lT_ready[b] = (hi, lo)

    qk_ready, en_done, at_ready, at_free, AT_ready = {}, {}, {}, {}, {}

    def project(b):
        pe.wait(c_in[b], w_in)
        toks = []
        for k, (w, o) in enumerate(((wqs, QT), (wks, KT))):
            bank = 6 + k
            pe.wait(*ps_free[bank])
            for c in range(2):
                s = pe.do(lambda g, w=w, c=c, bank=bank: g.matmul(PS[bank][:, :], w[:, c, :], cx[:, c, :],
                                                                  start=(c == 0), stop=(c == 1)),
                          "pe_pj" if c == 1 else None)
            act.wait(s, w_in, en_done.get(b - 1))
            t = act.do(lambda g, k=k, o=o, bank=bank: g.activation(o[:, :], PS[bank][:, :], ACT.Identity,
                                                                   bias=bqk[:, k:k + 1]), "act_qk")
            ps_free[bank] = (t,)
        ctx_free[b] = s
        qk_ready[b] = t

    def energy(b):
        pe.wait(qk_ready[b])
        for m in range(NTB):
            bank = 2 + m % 2
            pe.wait(*ps_free[bank])
            s = pe.do(lambda g, m=m, bank=bank: g.matmul(PS[bank][:, :], QT[:, m * P:(m + 1) * P], KT[:, :],
                                                         start=True, stop=True), "pe_en")
            dve.wait(s)
            t = dve.do(lambda g, m=m, bank=bank: g.tensor_reduce(sm[:, 0, m:m + 1], PS[bank][:, :], AX.X,
                                                                 ALU.max, negate=True), "dve_mx")
            act.wait(s, t, at_free.get(b - 1))
            a = act.do(lambda g, m=m, bank=bank: g.activation(At[:, m, :], PS[bank][:, :], ACT.Exp,
                                                              bias=sm[:, 0, m:m + 1], accum_out=sm[:, 1, m:m + 1]),
                       "act_ex")
            ps_free[bank] = (a,)
            dve.wait(a)
            t = dve.do(lambda g, m=m: g.reciprocal(sm[:, 2, m:m + 1], sm[:, 1, m:m + 1]), "dve_rc")
            dve.wait(t)
            t = dve.do(lambda g, m=m: g.tensor_scalar(At[:, m, :], At[:, m, :], sm[:, 2, m:m + 1], None,
                                                      ALU.mult), "dve_at")
            at_ready[b, m] = t
        en_done[b] = s

    def transpose_at(b):
        for m in range(NTB):
            k = t_bank()
            pe.wait(at_ready[b, m], *ps_free[k])
            for c in range(4):
                fn = lambda g, m=m, c=c, k=k: g.transpose(PS[k][:, c * P:(c + 1) * P],
                                                          At[:, m, c * P:(c + 1) * P], ident)
                s = pe.do(fn, "pe_ta" if c == 3 else None)
            src = PS[k][:, :].rearrange("p (c m) -> p c m", c=4)
            act.wait(s, xm_done.get(b - 1))
            hi = act.do(lambda g, m=m, src=src: g.activation(ATh[:, :, m * P:(m + 1) * P], src, ACT.Copy), "act_AT")
            dve.wait(s, hi)
            lo = dve.do(lambda g, m=m, src=src: g.tensor_tensor(
                ATl[:, :, m * P:(m + 1) * P], src, f32(ATh[:, :, m * P:(m + 1) * P]), ALU.subtract), "dve_AT")
            ps_free[k] = (hi, lo)
        at_free[b] = s
        AT_ready[b] = (hi, lo)

    x2_ready, ystore = {}, {}

    def mix(b):
        pe.wait(*AT_ready[b], *lT_ready[b])
        xb = xs[b % 2]
        for i in range(NTB):
            bank = 4 + i % 2
            pe.wait(*ps_free[bank])
            n = 0
            for c in range(4):
                for a, w in ((lTh, ATh), (lTh, ATl), (lTl, ATh)):
                    s = pe.do(lambda g, i=i, c=c, a=a, w=w, bank=bank, n=n: g.matmul(
                        PS[bank][:, :], a[:, c, i * P:(i + 1) * P], w[:, c, :], start=(n == 0), stop=(n == 11)),
                        "pe_xm" if n == 11 else None)
                    n += 1
            dve.wait(s, tg_ready)
            t = dve.do(lambda g, i=i, bank=bank: g.scalar_tensor_tensor(
                out=xb[:, i, :], in0=PS[bank][:, :], scalar=tgx, in1=xb[:, i, :], op0=ALU.mult, op1=ALU.add),
                "dve_x2")
            ps_free[bank] = (t,)
        xm_done[b] = s
        x2_ready[b] = t
        act.wait(t)
        stored[b] = dma(act, y[b * L:(b + 1) * L, :].rearrange("(i p) n -> p i n", p=P), xb[:, :, :], "out_x2")

    rowst, l2free, key_done = {}, [None], {}

    def layer2(b):
        r = norm_stats(1, xs[b % 2], [x2_ready[b]], b)
        dve.wait(r, rowst.get(b - 1), l2use.get(b - 1))
        for i in range(NTB):
            s = dve.do(lambda g, i=i: g.tensor_scalar(
                r2[:, i, 0:H].rearrange("p (k m) -> p k m", k=4),
                xs[b % 2][:, i, :].rearrange("p (m k) -> p k m", k=4), mv[:, 1, i, 0:1],
                rs[:, 1, 1, i:i + 1], ALU.subtract, ALU.mult), "dve_l2")
            l2_ready[b, i] = s
        x_free[b] = s

    l2_ready, l2use = {}, {}

    def route(b):
        for i in range(NTB):
            tile = b * NTB + i
            k = t_bank()
            pe.wait(l2_ready[b, i], *ps_free[k])
            for c in range(4):
                s = pe.do(lambda g, i=i, c=c, k=k: g.transpose(PS[k][:, c * P:(c + 1) * P],
                                                               r2[:, i, c * P:(c + 1) * P], ident),
                          "pe_t2" if c == 3 else None)
            act.wait(s, l2free[0])
            t = act.do(lambda g, k=k: g.activation(l2T[:, :, :], PS[k][:, :].rearrange("p (c m) -> p c m", c=4),
                                                   ACT.Copy), "act_l2")
            ps_free[k] = (t,)
            l2use[b] = s
            bank = 6 + i % 2
            pe.wait(t, gw_in, *ps_free[bank])
            for c in range(4):
                s = pe.do(lambda g, c=c, bank=bank: g.matmul(PS[bank][:, 0:E], l2T[:, c, :], gws[:, c, :],
                                                             start=(c == 0), stop=(c == 3)),
                          "pe_lg" if c == 3 else None)
            l2free[0] = s
            lg = PS[bank][:, 0:E]
            dve.wait(s, vr, score_free[0])
            t = dve.do(lambda g, lg=lg: g.max(v8[:, 0, :], lg), "dve_v8")
            dve.wait(t)
            dve.do(lambda g: g.tensor_scalar(sm[:, 3, 0:1], v8[:, 0, 0:1], -1.0, None, ALU.mult), "dve_nm")
            t = dve.do(lambda g: g.tensor_copy(v8[:, 1, 0:TOPK], v8[:, 0, 0:TOPK]), "dve_nm")
            act.wait(s, t, rowst.get(b - 1))
            a = act.do(lambda g, i=i, lg=lg: g.activation(r2[:, i, H:ROW], lg, ACT.Exp, bias=sm[:, 3, 0:1],
                                                          accum_out=sm[:, 4, 0:1]), "act_sc")
            dve.wait(t, a)
            t = dve.do(lambda g, lg=lg: g.match_replace(mr[:, :], v8[:, 1, :], lg, FOUND), "dve_mr")
            ps_free[bank] = (a, t)
            dve.wait(t, cst_in)
            key_done[tile] = dve.do(lambda g, tile=tile: g.tensor_scalar(
                KM[:, tile % 8, (tile // 8) * E:(tile // 8 + 1) * E], mr[:, :], FOUND, ktab[:, tile:tile + 1],
                ALU.is_equal, ALU.mult), "dve_km")
            dve.wait(a)
            t = dve.do(lambda g: g.reciprocal(sm[:, 5, 0:1], sm[:, 4, 0:1]), "dve_rr")
            dve.wait(t, tg_ready)
            t = dve.do(lambda g, i=i: g.tensor_scalar(r2[:, i, H:ROW], r2[:, i, H:ROW], sm[:, 5, 0:1], tgf,
                                                      ALU.mult, ALU.mult), "dve_sc")
            score_free[0] = t
        act.wait(t)
        rowst[b] = dma(act, rows[b * L:(b + 1) * L, :].rearrange("(i p) n -> p i n", p=P), r2[:, :, :], "out_rows")

    score_free = [None]

    layer1(0)
    project(0)
    transpose_ln(0)
    energy(0)
    for b in range(B):
        if b + 1 < B:
            load_ctx(b + 1)
            layer1(b + 1)
            project(b + 1)
        transpose_at(b)
        mix(b)
        if b + 1 < B:
            energy(b + 1)
        layer2(b)
        if b + 2 < B:
            load_x(b + 2)
        if b + 1 < B:
            transpose_ln(b + 1)
        route(b)

    act.wait(rowst[B - 1], ln_free[B - 1])
    z = act.do(lambda g: g.activation(lnx[:, 0:2, :], cs[:, 0:1].unsqueeze(2).to_broadcast([P, 2, H]), ACT.Copy,
                                      scale=0.0), "act_z")
    act.wait(z)
    ystore = dma(act, y[T:ROWS, :], lnx[:, 0, :], "out_z")
    ystore = dma(act, rows[T:ROWS, 0:H], lnx[:, 0, :], "out_z")
    ystore = dma(act, rows[T:ROWS, H:ROW], lnx[:, 1, 0:E], "out_z")

    pe.wait(key_done[NT - 1])
    key_ps = []
    for k in range(2):
        bank = 6 + k
        pe.wait(*ps_free[bank])
        for j in range(4):
            s = pe.do(lambda g, k=k, j=j, bank=bank: g.transpose(PS[bank][:, j * P:(j + 1) * P],
                                                                 KM[:, 4 * k + j, :], ident),
                      "pe_kt" if j == 3 else None)
        key_ps.append(s)
    for k in range(2):
        dve.wait(key_ps[k])
        t = dve.do(lambda g, k=k: g.tensor_copy(keyT[:, k * 512:(k + 1) * 512], PS[6 + k][:, :]), "dve_kt")
        ps_free[6 + k] = (t,)
    rounds = []
    last = [t]

    def round_of(src, out, r, more):
        def go():
            dve.wait(last[0])
            t = dve.do(lambda g: g.max(out[:, r * 8:(r + 1) * 8], src), "dve_rd")
            if more:
                dve.wait(t)
                t = dve.do(lambda g: g.match_replace(src, out[:, r * 8:(r + 1) * 8], src, 0.0), "dve_rd")
            last[0] = t
        return go

    for r in range(16):
        rounds.append((2.2, round_of(keyT[:, :], LA[:, :], r, r < 15)))

    def join():
        dve.wait(last[0])
        dve.do(lambda g: g.tensor_copy(L2[:, 0:P], LA[0:E, :]), "dve_jn")
        last[0] = dve.do(lambda g: g.tensor_copy(L2[:, P:2 * P], LA[E:P, :]), "dve_jn")

    rounds.append((0.4, join))
    for r in range(16):
        rounds.append((0.7, round_of(L2[:, :], LF[:, :], r, r < 15)))
    idx_ready = [None]

    def finish_lists():
        bank = 0
        pe.wait(last[0], *ps_free[bank])
        s = pe.do(lambda g: g.transpose(PS[bank][:, 0:E], LF[:, :], ident[0:E, 0:E]), "pe_ix")
        dve.wait(s)
        src = PS[bank][:, 0:E]
        dve.do(lambda g: g.tensor_scalar(t12[:, 0, :], src, 0.0, pcol, ALU.is_equal, ALU.mult), "dve_ix")
        t = dve.do(lambda g: g.tensor_scalar(t12[:, 1, :], src, -1.0, float(T), ALU.mult, ALU.add), "dve_ix")
        ps_free[bank] = (t,)
        dve.wait(t)
        idx_ready[0] = dve.do(lambda g: g.tensor_tensor(idx[:, :], t12[:, 0, :], t12[:, 1, :], ALU.add), "dve_ix")

    a_done = [at_free[B - 1], xm_done[B - 1], l2free[0], l2use[B - 1], key_ps[1], qk_ready[B - 1], z,
              score_free[0], key_done[NT - 1], x_free[B - 1], stored[B - 1], rowst[B - 1], ystore,
              AT_ready[B - 1][0], AT_ready[B - 1][1], gw_in, w_in, cst_in]

    jobs, lead = plan_jobs()
    NJ = len(jobs)
    job_of = {j[1]: n for n, j in enumerate(jobs) if j[0] == "e"}
    src_no, srcs = [], []
    for j in jobs:
        if j[0] == "e" or j[2] == 0:
            srcs.append(j)
        src_no.append(len(srcs) - 1)
    first_use = {}
    for n, s in enumerate(src_no):
        first_use.setdefault(s, n)

    xg_ready, xg_free, xT_ready, xT_free = {}, {}, {}, {}
    gu_done, h_ready, h_T, hT_ready, hT_free, d_done, ob_ready, acc_tok = {}, {}, {}, {}, {}, {}, {}, {}
    acc_chain = [None]
    ob_n = [0]
    d_free = {}

    for q in (act, dve, pool):
        q.wait(*a_done)
    PS_X, PS_H, PS_D = 0, 1, (6, 7)

    def gather(s):
        kind, k = srcs[s][0:2]
        pool.wait(*xg_free.get(s - NXG, ()), *(rowst[b] for b in range(B)), ystore)
        tag = f"xg{s % NXG}"
        if kind == "e":
            pool.wait(idx_ready[0])
            xg_ready[s] = pool.do(lambda g: g.indirect_dma_start(
                out=XG[s % NXG][:, :], out_offset=None, in_=rows[:, :],
                in_offset=bass.IndirectOffsetOnAxis(ap=idx[:, k:k + 1], axis=0)), tag, 16)
        else:
            xg_ready[s] = dma(pool, XG[s % NXG][:, :], rows[k * P:(k + 1) * P, :], tag)

    def x_transposes(s):
        pe.wait(xg_ready[s], *ps_free[PS_X])
        for c in range(4):
            t = pe.do(lambda g, c=c: g.transpose(PS[PS_X][:, c * P:(c + 1) * P],
                                                 XG[s % NXG][:, c * P:(c + 1) * P], ident),
                      "pe_tg" if c == 3 else None)
        xg_free[s] = (t,)
        act.wait(t, xT_free.get(s - 2))
        hi = act.do(lambda g: g.activation(xTh[s % 2][:, :], PS[PS_X][:, :], ACT.Copy), "act_xT")
        xT_ready[s] = (hi, t)

    def x_low(s):
        hi, t = xT_ready[s]
        dve.wait(t, hi, xT_free.get(s - 2))
        lo = dve.do(lambda g: g.tensor_tensor(xTl[s % 2][:, :], PS[PS_X][:, :], f32(xTh[s % 2][:, :]),
                                              ALU.subtract), "dve_xT")
        ps_free[PS_X] = (hi, lo)
        xT_ready[s] = (hi, lo)

    def wset(n):
        j = jobs[n]
        return j[2] if j[0] == "s" else 2 + j[1]

    def up(n):
        s, w = src_no[n], wset(n)
        wh, wl = dest(w)
        bg, bu = 2 + 2 * (n % 2), 3 + 2 * (n % 2)
        pe.wait(*xT_ready[s], *ps_free[bg], *ps_free[bu], *set_ready[w, "G"], *set_ready[w, "U"])
        h, l = xTh[s % 2], xTl[s % 2]
        k = 0
        for c in range(4):
            for a, w_ in ((h, wh), (h, wl), (l, wh)):
                for bank, o in ((bg, 0), (bu, GU)):
                    k += 1
                    t = pe.do(lambda g, a=a, w_=w_, c=c, bank=bank, o=o, k=k: g.matmul(
                        PS[bank][:, 0:F], a[:, c * P:(c + 1) * P], w_[:, o + c * F:o + (c + 1) * F],
                        start=(k <= 2), stop=(k > 22)), "pe_gu" if k == 24 else None)
        gu_done[n] = t
        if n + 1 == NJ or src_no[n + 1] != s:
            xT_free[s] = t
        for u in "GU":
            set_freed[w, u] = (t,)

    def silu(n):
        bg = 2 + 2 * (n % 2)
        act.wait(gu_done[n], h_ready.get(n - 1))
        t = act.do(lambda g: g.activation(sg_[0][:, :], PS[bg][:, 0:F], ACT.Silu), "act_si")
        return t

    def gate(n, si):
        bg, bu = 2 + 2 * (n % 2), 3 + 2 * (n % 2)
        dve.wait(gu_done[n], si, h_T.get(n - 1))
        t = dve.do(lambda g: g.tensor_tensor(hg[0][:, :], PS[bu][:, 0:F], sg_[0][:, :], ALU.mult), "dve_hg")
        h_ready[n] = t
        ps_free[bg] = (t,)
        ps_free[bu] = (t,)

    def h_transposes(n):
        pe.wait(h_ready[n], *ps_free[PS_H])
        for c in range(3):
            m = FKS[c]
            t = pe.do(lambda g, c=c, m=m: g.transpose(PS[PS_H][0:m, c * P:(c + 1) * P],
                                                      hg[0][:, c * P:c * P + m], ident),
                      "pe_th" if c == 2 else None)
        h_T[n] = t

    def h_high(n):
        act.wait(h_T[n], d_done.get(n - 1))
        act.do(lambda g: g.activation(hTh[0][:, 0:256], PS[PS_H][:, 0:256], ACT.Copy), "act_hT")
        hi = act.do(lambda g: g.activation(hTh[0][0:FKS[2], 256:384], PS[PS_H][0:FKS[2], 256:384], ACT.Copy),
                    "act_hT")
        return hi

    def h_low(n, hi):
        dve.wait(h_T[n], hi, d_done.get(n - 1))
        dve.do(lambda g: g.tensor_tensor(hTl[0][:, 0:256], PS[PS_H][:, 0:256], f32(hTh[0][:, 0:256]),
                                         ALU.subtract), "dve_hT")
        lo = dve.do(lambda g: g.tensor_tensor(hTl[0][0:FKS[2], 256:384], PS[PS_H][0:FKS[2], 256:384],
                                              f32(hTh[0][0:FKS[2], 256:384]), ALU.subtract), "dve_hT")
        ps_free[PS_H] = (hi, lo)
        hT_ready[n] = (hi, lo)

    def down(n):
        w, s = wset(n), src_no[n]
        wh, wl = dest(w)
        bank = PS_D[s % 2]
        first = jobs[n][0] == "e" or jobs[n][2] == 0
        final = jobs[n][0] == "e" or jobs[n][2] == 1
        pe.wait(*hT_ready[n], *set_ready[w, "D"])
        if first:
            pe.wait(*ps_free[bank])
        k = 0
        for c in range(3):
            m = FKS[c]
            o = 2 * GU + c * H
            for a, w_ in ((hTh[0], wh), (hTh[0], wl), (hTl[0], wh)):
                k += 1
                t = pe.do(lambda g, a=a, w_=w_, c=c, m=m, o=o, k=k: g.matmul(
                    PS[bank][:, :], a[0:m, c * P:(c + 1) * P], w_[0:m, o:o + H],
                    start=(k == 1 and first), stop=(k == 9 and final)), "pe_dn" if k == 9 else None)
        d_done[n] = t
        set_freed[w, "D"] = (t,)

    def scale_out(n):
        if not (jobs[n][0] == "e" or jobs[n][2] == 1):
            return
        s = src_no[n]
        i = ob_n[0]
        ob_n[0] += 1
        wcol = XG[s % NXG][:, H + jobs[n][1]:H + jobs[n][1] + 1] if jobs[n][0] == "e" else tgf
        act.wait(d_done[n], acc_tok.get(i - 2), xg_ready[s])
        t = act.do(lambda g: g.activation(ob[i % 2][:, :], PS[PS_D[s % 2]][:, :], ACT.Copy, scale=wcol), "act_ob")
        ps_free[PS_D[s % 2]] = (t,)
        xg_free[s] = (*xg_free[s], t)
        ob_ready[n] = (i, t)

    def accumulate(n):
        if n not in ob_ready:
            return
        i, t = ob_ready[n]
        pool.wait(t, acc_chain[0], *(stored[b] for b in range(B)), ystore)
        if jobs[n][0] == "e":
            e = jobs[n][1]
            tok = pool.do(lambda g: g.indirect_dma_start(
                out=y[:, :], out_offset=bass.IndirectOffsetOnAxis(ap=idx[:, e:e + 1], axis=0),
                in_=ob[i % 2][:, :], in_offset=None, compute_op=ALU.add), "acc", 16)
        else:
            k = jobs[n][1]
            tok = dma(pool, y[k * P:(k + 1) * P, :], ob[i % 2][:, :], "acc", accum_op=ALU.add)
        acc_chain[0] = tok
        acc_tok[i] = tok

    ahead = [(e, u) for e in range(E) for u in ("G", "U", "D")]
    ahead.sort(key=lambda k: (job_of[k[0]] - (0 if k[1] == "D" else 1), k[0]))
    per_step = 3 * E / (NJ - lead)

    def may(e, u, n):
        if e < 2:
            return n >= lead - 4 if e == 0 else n >= lead - 1
        return job_of[e - 2] + (1 if u == "D" else 0) <= n - 1

    def must(e, u, n):
        return n >= job_of[e] - (0 if u == "D" else 1)

    gathered = [0]

    def gather_to(n):
        while gathered[0] < len(srcs) and first_use[gathered[0]] <= n + 2:
            s = gathered[0]
            if s - NXG >= 0 and first_use[s - NXG] > n - 2 and n >= 0:
                pass
            if srcs[s][0] == "e" and idx_ready[0] is None:
                return
            if s - NXG >= 0 and scale_pending(s - NXG):
                return
            gather(s)
            gathered[0] += 1

    def scale_pending(s):
        lastn = max(n for n in range(first_use[s], min(first_use[s] + 2, NJ)) if src_no[n] == s)
        return lastn not in ob_ready

    gather_to(0)
    x_transposes(0)
    x_low(0)
    done_units = 0
    for n in range(NJ + 1):
        todo = []
        while ahead and n < NJ:
            e, u = ahead[0]
            if not may(e, u, n):
                assert not must(e, u, n), (e, u, n)
                break
            if not must(e, u, n) and done_units >= per_step * (n - lead + 4):
                break
            todo.append(ahead.pop(0))
            done_units += 1
        hi_h = h_high(n - 1) if n >= 1 else None
        if n >= 1:
            h_low(n - 1, hi_h)
        if n < NJ:
            up(n)

        def split(k):
            e, u = k
            if n < lead and e == 0:
                hi = split_high(pool, 2 + e, u, "pool_wh")
                split_low(pool, 2 + e, u, hi, "pool_wl")
            else:
                if e == 1:
                    for q in (act, dve):
                        q.wait(idx_ready[0])
                hi = split_high(act, 2 + e, u, "act_wh")
                split_low(dve, 2 + e, u, hi, "dve_wl")
            if e + 2 < E:
                load_raw(2 + e + 2, u)

        room = 4.6
        while rounds and (room > 0 or n == lead - 2):
            cost, go = rounds.pop(0)
            go()
            room -= cost
        if not rounds and idx_ready[0] is None:
            finish_lists()
        half = (len(todo) * 2 + 2) // 3
        for k in todo[:half]:
            split(k)
        if n < NJ:
            si = silu(n)
            gate(n, si)
        if n + 1 < NJ and src_no[n + 1] != src_no[n]:
            gather_to(n)
            x_transposes(src_no[n + 1])
            x_low(src_no[n + 1])
        if n >= 1:
            down(n - 1)
        if n < NJ:
            h_transposes(n)
        for k in todo[half:]:
            split(k)
        if n >= 1:
            scale_out(n - 1)
        gather_to(n)
        if n >= 1:
            accumulate(n - 1)
    pool.wait(acc_chain[0])

    with nc.Block() as block:
        @block.sync
        def _(g):
            sp.replay(g)

        @block.scalar
        def _(g):
            act.replay(g)

        @block.tensor
        def _(g):
            pe.replay(g)

        @block.vector
        def _(g):
            dve.replay(g)

        @block.gpsimd
        def _(g):
            pool.replay(g)
    ctx.close()


def kernel(x, ctx_1024, g_xattn, g_ffn, L0_xattn_Wq, L0_xattn_bq, L0_xattn_Wk, L0_xattn_bk, L0_ffn_gate_w,
           L0_ffn_w_gate, L0_ffn_w_up, L0_ffn_w_down, L0_ffn_sh_gate, L0_ffn_sh_up, L0_ffn_sh_down):
    import numpy as np
    import concourse.bacc as bacc
    from concourse import mybir as mb
    from concourse.bass_utils import run_bass_kernel_spmd

    nc = bacc.Bacc("TRN2", target_bir_lowering=False, num_devices=1)
    cst = np.zeros((P, 145), np.float32)
    cst[:, 0:128] = np.eye(P, dtype=np.float32)
    for t in range(NT):
        cst[:, 128 + t] = T - (P * t + np.arange(P))
    cst[:, 144] = np.arange(P)
    c = np.ascontiguousarray
    arrays = {
        "x": c(x), "ctxt": c(np.transpose(np.asarray(ctx_1024), (0, 2, 1))),
        "gx": c(np.asarray(g_xattn).reshape(1, 1)), "gf": c(np.asarray(g_ffn).reshape(1, 1)),
        "wq": c(np.asarray(L0_xattn_Wq).T), "bq": c(np.asarray(L0_xattn_bq).reshape(D, 1)),
        "wk": c(np.asarray(L0_xattn_Wk).T), "bk": c(np.asarray(L0_xattn_bk).reshape(D, 1)),
        "gw": c(np.asarray(L0_ffn_gate_w).T), "wg": c(L0_ffn_w_gate), "wu": c(L0_ffn_w_up), "wd": c(L0_ffn_w_down),
        "sg": c(np.asarray(L0_ffn_sh_gate).T), "su": c(np.asarray(L0_ffn_sh_up).T),
        "sd": c(np.asarray(L0_ffn_sh_down).T), "cst": cst,
    }
    args = [nc.dram_tensor(f"i_{n}", a.shape, mb.dt.from_np(a.dtype), kind="ExternalInput").ap()
            for n, a in arrays.items()]
    y = nc.dram_tensor("o_y", (ROWS, H), FP, kind="ExternalOutput").ap()
    rows = nc.dram_tensor("rows", (ROWS, ROW), FP, kind="Internal").ap()
    build(nc, *args, y, rows)
    r = run_bass_kernel_spmd(nc, [{f"i_{n}": a for n, a in arrays.items()}], core_ids=[0])
    return r.results[0]["o_y"][0:T].reshape(B, L, H)
```

```python
import concourse.bass as bass
from concourse import mybir
from contextlib import ExitStack

P = 128
B, L, H, C, D = 4, 512, 512, 256, 128
T = B * L
E, F, TOPK, CAP = 64, 352, 6, 128
NT = T // P
NTB = L // P
FSH = 2 * F
ROW = H + E
GU = 4 * F
WALL = 2 * GU + 3 * H
ROWS = T + P
EPS = 1e-5

FP = mybir.dt.float32
FR = mybir.dt.float32r
I32 = mybir.dt.int32
ALU = mybir.AluOpType
ACT = mybir.ActivationFunctionType
AX = mybir.AxisListType
FOUND = -2.0e38
ABSENT = 3.0e38

FKS = [128, 128, F - 256]


LEAD = 4
ROOM = 5.6
SLACK = 4
QUOTA = 3


def plan_jobs():
    halves = [("s", t, h) for t in range(NT) for h in range(2)]
    jobs, rest = halves[:2 * LEAD], halves[2 * LEAD:]
    n = len(rest)
    for e in range(E):
        jobs.append(("e", e, 0))
        if rest and (e + 1) * n // (E - 3) > n - len(rest):
            jobs.append(rest.pop(0))
    assert not rest
    return jobs, 2 * LEAD


class Queue:

    def __init__(self, book):
        self.book, self.steps, self.seen = book, [], {}

    def wait(self, *toks):
        for tok in toks:
            if tok is None:
                continue
            name, val = tok
            if self.seen.get(name, 0) < val:
                self.seen[name] = val
                sem = self.book.sem(name)
                self.steps.append(lambda eng, s=sem, v=val: eng.wait_ge(s, v))

    def do(self, fn, tag=None, by=1):
        if tag is None:
            self.steps.append(fn)
            return None
        tok = self.book.tick(tag, by)
        sem = self.book.sem(tag)
        self.steps.append(lambda eng: fn(eng).then_inc(sem, by))
        return tok

    def replay(self, eng):
        for s in self.steps:
            s(eng)


class Book:

    def __init__(self, nc, ctx):
        self.nc, self.ctx, self.sems, self.count = nc, ctx, {}, {}

    def sem(self, name):
        if name not in self.sems:
            self.sems[name] = self.ctx.enter_context(self.nc.semaphore(name))
        return self.sems[name]

    def tick(self, name, by):
        self.count[name] = self.count.get(name, 0) + by
        return (name, self.count[name])


def build(nc, x, ctxt, gx, gf, wq, bq, wk, bk, gw, wg, wu, wd, sg, su, sd, cst, y, rows):
    ctx = ExitStack()
    book = Book(nc, ctx)
    sp, act, pe, dve, pool = (Queue(book) for _ in range(5))

    def sb(stack, name, shape, dt=FP):
        return stack.enter_context(nc.sbuf_tensor(name, shape, dt))

    jobs, lead = plan_jobs()
    NJ = len(jobs)

    cs = sb(ctx, "cs", [P, 128 + 16 + 1])
    ident, ktab, pcol = cs[:, 0:128], cs[:, 128:144], cs[:, 144:145]
    SWH = [sb(ctx, f"SWH{s}", [P, WALL], FR) for s in range(2)]
    SWL = [sb(ctx, f"SWL{s}", [P, WALL], FR) for s in range(2)]
    RW = [sb(ctx, f"RW{s}", [P, WALL]) for s in range(2)]
    idx = sb(ctx, "idx", [P, E], I32)
    tg2 = sb(ctx, "tg2", [P, 4])
    tgx, tgf = tg2[:, 2:3], tg2[:, 3:4]
    tiny = sb(ctx, "tiny", [P, 64])

    PS = [ctx.enter_context(nc.psum_tensor(f"PS{i}", [P, 512], FP)) for i in range(8)]

    actx = ExitStack()
    xs = [sb(actx, f"xs{i}", [P, NTB, H]) for i in range(2)]
    cxs = [sb(actx, f"cx{i}", [P, 2, L]) for i in range(2)]
    wqs = sb(actx, "wqs", [P, 2, D])
    wks = sb(actx, "wks", [P, 2, D])
    bqk = sb(actx, "bqk", [P, 2])
    gws = sb(actx, "gws", [P, 4, E])
    lnx = sb(actx, "lnx", [P, NTB, H])
    lTh = sb(actx, "lTh", [P, 4, L], FR)
    lTl = sb(actx, "lTl", [P, 4, L], FR)
    QT = sb(actx, "QT", [P, L])
    KT = sb(actx, "KT", [P, L])
    At = sb(actx, "At", [P, NTB, L])
    ATh = sb(actx, "ATh", [P, 4, L], FR)
    ATl = sb(actx, "ATl", [P, 4, L], FR)
    l2T = sb(actx, "l2T", [P, 2, 4, P])
    r2 = sb(actx, "r2", [P, NTB, ROW])
    st = sb(actx, "st", [P, 2, NTB, 6])
    mv = sb(actx, "mv", [P, 2, NTB, 2])
    rs = sb(actx, "rs", [P, 2, 4, NTB])
    sm = sb(actx, "sm", [P, 3, NTB])
    v8 = sb(actx, "v8", [P, 2, 2, 8])
    mr = sb(actx, "mr", [P, 2, E])
    rt = sb(actx, "rt", [P, 2, 4])
    KM = sb(actx, "KM", [P, 8, 2 * E])
    keyT = sb(actx, "keyT", [P, 1024])
    LA = sb(actx, "LA", [P, P])
    L2 = sb(actx, "L2", [E, 2 * P])
    LF = sb(actx, "LF", [E, P])
    t12 = sb(actx, "t12", [P, 2, E])
    actx.close()

    WH, WL = [None, None], [None, None]
    WH[0], WL[0] = sb(ctx, "WH0", [P, WALL], FR), sb(ctx, "WL0", [P, WALL], FR)
    NXG = 3
    XG = [sb(ctx, f"XG{i}", [P, ROW]) for i in range(NXG)]
    xTh = [sb(ctx, f"xTh{i}", [P, 512], FR) for i in range(3)]
    xTl = [sb(ctx, f"xTl{i}", [P, 512], FR) for i in range(3)]
    sg_ = [sb(ctx, f"sgl{i}", [P, F]) for i in range(1)]
    hg = [sb(ctx, f"hg{i}", [P, 384]) for i in range(1)]
    hTh = [sb(ctx, f"hTh{i}", [P, 384], FR) for i in range(1)]
    hTl = [sb(ctx, f"hTl{i}", [P, 384], FR) for i in range(1)]
    ob = [sb(ctx, f"ob{i}", [P, H]) for i in range(2)]
    WH[1], WL[1] = sb(ctx, "WH1", [P, WALL], FR), sb(ctx, "WL1", [P, WALL], FR)

    f32 = lambda ap: ap.bitcast(FP)
    dma = lambda q, out, in_, tag, **kw: q.do(lambda g: g.dma_start(out, in_, **kw), tag, 16)

    def load_x(b):
        sp.wait(x_free.get(b - 2), stored.get(b - 2))
        x_in[b] = dma(sp, xs[b % 2][:, :, :], x[b].rearrange("(i p) n -> p i n", p=P), f"in_x{b % 2}")

    def load_ctx(b):
        sp.wait(ctx_free.get(b - 2))
        c_in[b] = dma(sp, cxs[b % 2][:, :, :], ctxt[b].rearrange("(k p) n -> p k n", p=P), f"in_ctx{b % 2}")

    x_in, c_in, x_free, ctx_free, stored = {}, {}, {}, {}, {}
    load_x(0)
    load_ctx(0)
    for o, i in ((wqs, wq), (wks, wk)):
        w_in = dma(sp, o[:, :, :], i.rearrange("(k p) d -> p k d", p=P), "in_w")
    w_in = dma(sp, bqk[:, 0:1], bq, "in_w")
    w_in = dma(sp, bqk[:, 1:2], bk, "in_w")
    cst_in = dma(act, cs[:, :], cst, "in_cst")
    g_in = dma(act, tg2[:, 0:1], gx.to_broadcast([P, 1]), "in_g")
    g_in = dma(act, tg2[:, 1:2], gf.to_broadcast([P, 1]), "in_g")
    gw_in = dma(act, gws[:, :, :], gw.rearrange("(p k) e -> p k e", k=4), "in_gw")
    raw_in, raw_free = {}, {}

    def unit(u):
        return slice({"G": 0, "U": GU, "D": 2 * GU}[u], {"G": GU, "U": 2 * GU, "D": WALL}[u])

    def load_raw(n, u):
        t = RW[n % 2]
        sp.wait(*raw_free.get((n - 2, u), ()))
        if n < 2:
            cols = slice(n * F, (n + 1) * F)
            g_, u_, d_ = sg[:, cols], su[:, cols], sd[n * F:(n + 1) * F, :]
        else:
            g_, u_, d_ = wg[n - 2], wu[n - 2], wd[n - 2]
        tag = f"raw{u}{n % 2}"
        if u in "GU":
            src = (g_ if u == "G" else u_).rearrange("(p k) f -> p k f", k=4)
            tok = dma(sp, t[:, unit(u)].rearrange("p (k f) -> p k f", k=4), src, tag)
        else:
            o = 2 * GU
            dma(sp, t[:, o:o + 2 * H].rearrange("p (k n) -> p k n", k=2),
                d_[0:256, :].rearrange("(k p) n -> p k n", p=P), tag)
            tok = dma(sp, t[0:FKS[2], o + 2 * H:o + 3 * H], d_[256:F, :], tag)
        raw_in[n, u] = tok

    load_raw(0, "G")
    load_x(1)

    set_ready, set_freed = {}, {}

    def pieces(u):
        if u in "GU":
            s = unit(u)
            return [(P, s.start, s.stop)]
        o = 2 * GU
        return [(P, o, o + 2 * H), (FKS[2], o + 2 * H, o + 3 * H)]

    def dest(n):
        return (SWH[n], SWL[n]) if n < 2 else (WH[n % 2], WL[n % 2])

    def split_high(q, n, u, what):
        h, _ = dest(n)
        q.wait(raw_in[n, u], *set_freed.get((n - 2, u), ()))
        for np_, a, b in pieces(u):
            if q is act:
                fn = lambda g, np_=np_, a=a, b=b: g.activation(h[0:np_, a:b], RW[n % 2][0:np_, a:b], ACT.Copy)
            else:
                fn = lambda g, np_=np_, a=a, b=b: g.tensor_copy(h[0:np_, a:b], RW[n % 2][0:np_, a:b])
            tok = q.do(fn, what)
        return tok

    def split_low(q, n, u, high, what):
        h, l = dest(n)
        q.wait(raw_in[n, u], *set_freed.get((n - 2, u), ()), high)
        for np_, a, b in pieces(u):
            tok = q.do(lambda g, np_=np_, a=a, b=b: g.tensor_tensor(
                l[0:np_, a:b], RW[n % 2][0:np_, a:b], f32(h[0:np_, a:b]), ALU.subtract), what)
        raw_free[n, u] = (tok,)
        set_ready[n, u] = (high, tok)

    shared_units = [(n, u) for n in range(2) for u in "GUD"]

    def split_shared(k):
        for n, u in shared_units[0:k]:
            hi = split_high(act, n, u, "act_wh")
            split_low(pool, n, u, hi, "pool_wl")
            early.append((2 + n, u))
        del shared_units[0:k]

    early = []

    def load_early():
        while early:
            load_raw(*early.pop(0))

    act.wait(g_in)
    tg_ready = act.do(lambda g: g.activation(tg2[:, 2:4], tg2[:, 0:2], ACT.Tanh), "act_tg")
    vr = dve.do(lambda g: g.memset(v8[:, :, 1, :], ABSENT), "dve_vr")
    nh = pool.do(lambda g: g.memset(rs[:, 0, 3, :], -0.5), "pool_nh")
    nh = pool.do(lambda g: g.memset(rs[:, 1, 3, :], -0.5), "pool_nh")

    ps_free = [() for _ in range(8)]

    def bn(w, src, i):
        return dve.do(lambda g: g.bn_stats(st[:, w, i, :], src[:, i, :]), "dve_st")

    def rstd(w, s):
        dve.wait(s)
        for i in range(NTB):
            s = dve.do(lambda g, i=i: g.bn_aggr(mv[:, w, i, :], st[:, w, i, :]), "dve_mv")
        pool.wait(s, nh)
        ve, r, t = (rs[:, w, k, :] for k in range(3))
        s = pool.do(lambda g: g.tensor_scalar(ve, mv[:, w, :, 1], EPS, None, ALU.add), "pool_rs")
        pool.wait(s)
        s = pool.do(lambda g: g.tensor_tensor(r, ve, rs[:, w, 3, :], ALU.pow), "pool_rs")
        pool.wait(s)
        s = pool.do(lambda g: g.tensor_tensor(t, r, r, ALU.mult), "pool_rs")
        pool.wait(s)
        s = pool.do(lambda g: g.tensor_tensor(t, t, ve, ALU.mult), "pool_rs")
        pool.wait(s)
        s = pool.do(lambda g: g.tensor_scalar(t, t, -0.5, 1.5, ALU.mult, ALU.add), "pool_rs")
        pool.wait(s)
        s = pool.do(lambda g: g.tensor_tensor(r, r, t, ALU.mult), "pool_rs")
        return s

    ln_free, ln_done, T_use = {}, {}, [0]

    rs1 = {}

    def stats1(b):
        dve.wait(x_in[b])
        for i in range(NTB):
            s = bn(0, xs[b % 2], i)
        rs1[b] = rstd(0, s)

    def apply1(b):
        dve.wait(rs1[b], ln_free.get(b - 1))
        for i in range(NTB):
            s = dve.do(lambda g, i=i: g.tensor_scalar(lnx[:, i, :], xs[b % 2][:, i, :], mv[:, 0, i, 0:1],
                                                      rs[:, 0, 1, i:i + 1], ALU.subtract, ALU.mult), "dve_ln")
        ln_done[b] = s

    def t_bank(banks=(0, 4, 1, 5)):
        k = banks[T_use[0] % len(banks)]
        T_use[0] += 1
        return k

    lT_ready, xm_done = {}, {}

    def transpose_ln(b):
        pe.wait(ln_done[b], cst_in)
        for i in range(NTB):
            k = t_bank()
            pe.wait(*ps_free[k])
            for c in range(4):
                fn = lambda g, i=i, c=c, k=k: g.transpose(PS[k][:, c * P:(c + 1) * P],
                                                          lnx[:, i, c * P:(c + 1) * P], ident)
                s = pe.do(fn, "pe_tx" if c == 3 else None)
            act.wait(s, xm_done.get(b - 1))
            src = PS[k][:, :].rearrange("p (c m) -> p c m", c=4)
            hi = act.do(lambda g, i=i, src=src: g.activation(lTh[:, :, i * P:(i + 1) * P], src, ACT.Copy), "act_lT")
            dve.wait(s, hi, xm_done.get(b - 1))
            lo = dve.do(lambda g, i=i, src=src: g.tensor_tensor(
                lTl[:, :, i * P:(i + 1) * P], src, f32(lTh[:, :, i * P:(i + 1) * P]), ALU.subtract), "dve_lT")
            ps_free[k] = (hi, lo)
        ln_free[b] = s
        lT_ready[b] = (hi, lo)

    qk_ready, en_done, at_ready, at_free, AT_ready = {}, {}, {}, {}, {}

    def project(b):
        pe.wait(c_in[b], w_in)
        toks = []
        for k, (w, o) in enumerate(((wqs, QT), (wks, KT))):
            bank = 6 + k
            pe.wait(*ps_free[bank])
            for c in range(2):
                s = pe.do(lambda g, w=w, c=c, bank=bank: g.matmul(PS[bank][:, :], w[:, c, :], cxs[b % 2][:, c, :],
                                                                  start=(c == 0), stop=(c == 1)),
                          "pe_pj" if c == 1 else None)
            act.wait(s, w_in, en_done.get(b - 1))
            t = act.do(lambda g, k=k, o=o, bank=bank: g.activation(o[:, :], PS[bank][:, :], ACT.Identity,
                                                                   bias=bqk[:, k:k + 1]), "act_qk")
            ps_free[bank] = (t,)
        ctx_free[b] = s
        qk_ready[b] = t

    def energy(b):
        pe.wait(qk_ready[b])

        def normalise(m, a):
            dve.wait(a)
            t = dve.do(lambda g: g.reciprocal(sm[:, 2, m:m + 1], sm[:, 1, m:m + 1]), "dve_rc")
            dve.wait(t)
            at_ready[b, m] = dve.do(lambda g: g.tensor_scalar(At[:, m, :], At[:, m, :], sm[:, 2, m:m + 1], None,
                                                              ALU.mult), "dve_at")

        a = None
        for m in range(NTB):
            bank = 2 + m % 2
            pe.wait(*ps_free[bank])
            s = pe.do(lambda g, m=m, bank=bank: g.matmul(PS[bank][:, :], QT[:, m * P:(m + 1) * P], KT[:, :],
                                                         start=True, stop=True), "pe_en")
            dve.wait(s)
            t = dve.do(lambda g, m=m, bank=bank: g.tensor_reduce(sm[:, 0, m:m + 1], PS[bank][:, :], AX.X,
                                                                 ALU.max, negate=True), "dve_mx")
            if a:
                normalise(m - 1, a)
            act.wait(s, t, at_free.get(b - 1))
            a = act.do(lambda g, m=m, bank=bank: g.activation(At[:, m, :], PS[bank][:, :], ACT.Exp,
                                                              bias=sm[:, 0, m:m + 1], accum_out=sm[:, 1, m:m + 1]),
                       "act_ex")
            ps_free[bank] = (a,)
        normalise(NTB - 1, a)
        en_done[b] = s

    def transpose_at(b):
        for m in range(NTB):
            k = t_bank()
            pe.wait(at_ready[b, m], *ps_free[k])
            for c in range(4):
                fn = lambda g, m=m, c=c, k=k: g.transpose(PS[k][:, c * P:(c + 1) * P],
                                                          At[:, m, c * P:(c + 1) * P], ident)
                s = pe.do(fn, "pe_ta" if c == 3 else None)
            src = PS[k][:, :].rearrange("p (c m) -> p c m", c=4)
            act.wait(s, xm_done.get(b - 1))
            hi = act.do(lambda g, m=m, src=src: g.activation(ATh[:, :, m * P:(m + 1) * P], src, ACT.Copy), "act_AT")
            dve.wait(s, hi)
            lo = dve.do(lambda g, m=m, src=src: g.tensor_tensor(
                ATl[:, :, m * P:(m + 1) * P], src, f32(ATh[:, :, m * P:(m + 1) * P]), ALU.subtract), "dve_AT")
            ps_free[k] = (hi, lo)
        at_free[b] = s
        AT_ready[b] = (hi, lo)

    x2_ready, ystore = {}, {}

    def mix(b):
        xb = xs[b % 2]
        for i in range(NTB):
            if b:
                route_transpose(b - 1, i)
            bank = 4 + i % 2
            pe.wait(*AT_ready[b], *lT_ready[b])
            pe.wait(*ps_free[bank])
            n = 0
            for c in range(4):
                for a, w in ((lTh, ATh), (lTh, ATl), (lTl, ATh)):
                    s = pe.do(lambda g, i=i, c=c, a=a, w=w, bank=bank, n=n: g.matmul(
                        PS[bank][:, :], a[:, c, i * P:(i + 1) * P], w[:, c, :], start=(n == 0), stop=(n == 11)),
                        "pe_xm" if n == 11 else None)
                    n += 1
            if b:
                route_logits(b - 1, i)
            dve.wait(s, tg_ready)
            t = dve.do(lambda g, i=i, bank=bank: g.scalar_tensor_tensor(
                out=xb[:, i, :], in0=PS[bank][:, :], scalar=tgx, in1=xb[:, i, :], op0=ALU.mult, op1=ALU.add),
                "dve_x2")
            ps_free[bank] = (t,)
            if b:
                route_top(b - 1, i)
            dve.wait(t)
            x2_ready[b] = bn(1, xb, i)
            if b:
                route_score(b - 1, i)
            if i == 1 and b + 1 < B:
                apply1(b + 1)
            if i in (1, 3):
                split_shared(1)
        xm_done[b] = s
        act.wait(t)
        stored[b] = dma(act, y[b * L:(b + 1) * L, :].rearrange("(i p) n -> p i n", p=P), xb[:, :, :], f"out_x{b % 2}")

    rowst, key_done, l2_ready, lg_done, t2_done, score_done, tops = {}, {}, {}, {}, {}, {}, {}

    def layer2(b):
        dve.wait(rs2[b])
        for i in range(NTB):
            tile = b * NTB + i
            dve.wait(rowst.get(tile - NTB), t2_done.get(tile - NTB))
            s = dve.do(lambda g, i=i: g.tensor_scalar(
                r2[:, i, 0:H].rearrange("p (k m) -> p k m", k=4),
                xs[b % 2][:, i, :].rearrange("p (m k) -> p k m", k=4), mv[:, 1, i, 0:1],
                rs[:, 1, 1, i:i + 1], ALU.subtract, ALU.mult), "dve_l2")
            l2_ready[b, i] = s
        x_free[b] = s

    def route_transpose(b, i):
        tile = b * NTB + i
        k = t_bank((0, 1))
        pe.wait(l2_ready[b, i], *ps_free[k])
        for c in range(4):
            s = pe.do(lambda g, c=c: g.transpose(PS[k][:, c * P:(c + 1) * P], r2[:, i, c * P:(c + 1) * P], ident),
                      "pe_t2" if c == 3 else None)
        t2_done[tile] = s
        act.wait(s, lg_done.get(tile - 2))
        t = act.do(lambda g: g.activation(l2T[:, tile % 2, :, :], PS[k][:, :].rearrange("p (c m) -> p c m", c=4),
                                          ACT.Copy), "act_l2")
        ps_free[k] = (t,)

    def route_logits(b, i):
        tile = b * NTB + i
        bank = 6 + tile % 2
        pe.wait(("act_l2", book.count["act_l2"]), gw_in, *ps_free[bank])
        for c in range(4):
            s = pe.do(lambda g, c=c: g.matmul(PS[bank][:, 0:E], l2T[:, tile % 2, c, :], gws[:, c, :],
                                              start=(c == 0), stop=(c == 3)), "pe_lg" if c == 3 else None)
        lg_done[tile] = s

    def route_top(b, i):
        tile = b * NTB + i
        j = tile % 2
        bank = 6 + tile % 2
        lg = PS[bank][:, 0:E]
        dve.wait(lg_done[tile], vr, score_done.get(tile - 2))
        t = dve.do(lambda g: g.max(v8[:, j, 0, :], lg), "dve_v8")
        dve.wait(t)
        dve.do(lambda g: g.tensor_scalar(rt[:, j, 0:1], v8[:, j, 0, 0:1], -1.0, None, ALU.mult), "dve_nm")
        t = dve.do(lambda g: g.tensor_copy(v8[:, j, 1, 0:TOPK], v8[:, j, 0, 0:TOPK]), "dve_nm")
        act.wait(lg_done[tile], t, rowst.get(tile - NTB))
        a = act.do(lambda g: g.activation(r2[:, i, H:ROW], lg, ACT.Exp, bias=rt[:, j, 0:1],
                                          accum_out=rt[:, j, 1:2]), "act_sc")
        tops[tile] = (t, a)

    def route_score(b, i):
        tile = b * NTB + i
        j = tile % 2
        bank = 6 + tile % 2
        t, a = tops[tile]
        dve.wait(t, a)
        dve.do(lambda g: g.reciprocal(rt[:, j, 2:3], rt[:, j, 1:2]), "dve_mr")
        t = dve.do(lambda g: g.match_replace(mr[:, j, :], v8[:, j, 1, :], PS[bank][:, 0:E], FOUND), "dve_mr")
        ps_free[bank] = (a, t)
        dve.wait(t, cst_in, tg_ready)
        key_done[tile] = dve.do(lambda g: g.tensor_scalar(
            KM[:, tile % 8, (tile // 8) * E:(tile // 8 + 1) * E], mr[:, j, :], FOUND, ktab[:, tile:tile + 1],
            ALU.is_equal, ALU.mult), "dve_km")
        t = dve.do(lambda g: g.tensor_scalar(r2[:, i, H:ROW], r2[:, i, H:ROW], rt[:, j, 2:3], tgf,
                                             ALU.mult, ALU.mult), "dve_sc")
        score_done[tile] = t
        sp.wait(t)
        rowst[tile] = dma(sp, rows[tile * P:(tile + 1) * P, :], r2[:, i, :], f"out_row{i}")

    rs2 = {}
    load_ctx(1)
    for n in range(2):
        for u in "GUD":
            if n or u != "G":
                load_raw(n, u)
    project(0)
    stats1(0)
    energy(0)
    apply1(0)
    transpose_ln(0)
    project(1)
    split_shared(1)
    for b in range(B):
        if b + 2 < B:
            load_ctx(b + 2)
        transpose_at(b)
        if b + 1 < B:
            energy(b + 1)
            stats1(b + 1)
        mix(b)
        rs2[b] = rstd(1, x2_ready[b])
        if b + 2 < B:
            project(b + 2)
        if b + 1 < B:
            transpose_ln(b + 1)
        layer2(b)
        if b + 2 < B:
            load_x(b + 2)
        load_early()
    load_early()
    for i in range(NTB):
        route_transpose(B - 1, i)
        route_logits(B - 1, i)
        route_top(B - 1, i)
        route_score(B - 1, i)

    act.wait(ln_free[B - 1])
    z = act.do(lambda g: g.activation(lnx[:, 0:2, :], cs[:, 0:1].unsqueeze(2).to_broadcast([P, 2, H]), ACT.Copy,
                                      scale=0.0), "act_z")
    act.wait(z)
    ystore = dma(act, y[T:ROWS, :], lnx[:, 0, :], "out_z")
    ystore = dma(act, rows[T:ROWS, 0:H], lnx[:, 0, :], "out_z")
    ystore = dma(act, rows[T:ROWS, H:ROW], lnx[:, 1, 0:E], "out_z")

    pe.wait(key_done[NT - 1])
    key_ps = []
    for k in range(2):
        bank = 6 + k
        pe.wait(*ps_free[bank])
        for j in range(4):
            s = pe.do(lambda g, k=k, j=j, bank=bank: g.transpose(PS[bank][:, j * P:(j + 1) * P],
                                                                 KM[:, 4 * k + j, :], ident),
                      "pe_kt" if j == 3 else None)
        key_ps.append(s)
    for k in range(2):
        dve.wait(key_ps[k])
        t = dve.do(lambda g, k=k: g.tensor_copy(keyT[:, k * 512:(k + 1) * 512], PS[6 + k][:, :]), "dve_kt")
        ps_free[6 + k] = (t,)
    rounds = []
    last = [t]

    def round_of(src, out, r, more):
        def go():
            dve.wait(last[0])
            t = dve.do(lambda g: g.max(out[:, r * 8:(r + 1) * 8], src), "dve_rd")
            if more:
                dve.wait(t)
                t = dve.do(lambda g: g.match_replace(src, out[:, r * 8:(r + 1) * 8], src, 0.0), "dve_rd")
            last[0] = t
        return go

    for r in range(16):
        rounds.append((2.2, round_of(keyT[:, :], LA[:, :], r, r < 15)))

    def join():
        dve.wait(last[0])
        dve.do(lambda g: g.tensor_copy(L2[:, 0:P], LA[0:E, :]), "dve_jn")
        last[0] = dve.do(lambda g: g.tensor_copy(L2[:, P:2 * P], LA[E:P, :]), "dve_jn")

    rounds.append((0.4, join))
    for r in range(16):
        rounds.append((0.7, round_of(L2[:, :], LF[:, :], r, r < 15)))
    idx_ready = [None]

    def finish_lists():
        bank = 0
        pe.wait(last[0], *ps_free[bank])
        s = pe.do(lambda g: g.transpose(PS[bank][:, 0:E], LF[:, :], ident[0:E, 0:E]), "pe_ix")
        dve.wait(s)
        src = PS[bank][:, 0:E]
        dve.do(lambda g: g.tensor_scalar(t12[:, 0, :], src, 0.0, pcol, ALU.is_equal, ALU.mult), "dve_ix")
        t = dve.do(lambda g: g.tensor_scalar(t12[:, 1, :], src, -1.0, float(T), ALU.mult, ALU.add), "dve_ix")
        ps_free[bank] = (t,)
        dve.wait(t)
        idx_ready[0] = dve.do(lambda g: g.tensor_tensor(idx[:, :], t12[:, 0, :], t12[:, 1, :], ALU.add), "dve_ix")

    a_done = [at_free[B - 1], xm_done[B - 1], lg_done[NT - 1], key_ps[1], qk_ready[B - 1], z,
              score_done[NT - 1], x_free[B - 1], stored[B - 1], *(rowst[NT - 1 - i] for i in range(NTB)), ystore,
              AT_ready[B - 1][0], AT_ready[B - 1][1], gw_in, w_in, cst_in]

    job_of = {j[1]: n for n, j in enumerate(jobs) if j[0] == "e"}
    srcs = [j for j in jobs if j[2] == 0]
    src_no = [srcs.index((j[0], j[1], 0)) for j in jobs]
    first_use = {s: src_no.index(s) for s in range(len(srcs))}
    last_use = {s: n for n, s in enumerate(src_no)}
    place = [j[1] % 2 if j[0] == "e" else (2, 0, 1)[j[1] % 3] if j[1] < LEAD else 2 for j in srcs]
    dbank = [6 if j[0] == "e" else 6 + j[1] % 2 if j[1] < LEAD else 7 for j in srcs]

    xg_ready, xg_free, xT_ready, xT_free = {}, {}, {}, {}
    gu_done, h_ready, h_T, hT_ready, hT_free, d_done, ob_ready, acc_tok = {}, {}, {}, {}, {}, {}, {}, {}
    acc_chain = [None]
    ob_n = [0]
    d_free = {}

    for q in (act, dve, pool):
        q.wait(*a_done)
    PS_X, PS_H = 0, 1
    hg_pad = dve.do(lambda g: g.memset(hg[0][:, F:384], 0.0), "dve_pad")

    def gather(s):
        kind, k = srcs[s][0:2]
        pool.wait(*xg_free.get(s - NXG, ()), *(rowst[NT - 1 - i] for i in range(NTB)), ystore)
        tag = f"xg{s % NXG}"
        if kind == "e":
            pool.wait(idx_ready[0])
            xg_ready[s] = pool.do(lambda g: g.indirect_dma_start(
                out=XG[s % NXG][:, :], out_offset=None, in_=rows[:, :],
                in_offset=bass.IndirectOffsetOnAxis(ap=idx[:, k:k + 1], axis=0)), tag, 16)
        else:
            xg_ready[s] = dma(pool, XG[s % NXG][:, :], rows[k * P:(k + 1) * P, :], tag)

    def x_transposes(s):
        before = [r for r in range(s) if place[r] == place[s]]
        assert all(last_use[r] < first_use[s] for r in before)
        pe.wait(xg_ready[s], *ps_free[PS_X])
        for c in range(4):
            t = pe.do(lambda g, c=c: g.transpose(PS[PS_X][:, c * P:(c + 1) * P],
                                                 XG[s % NXG][:, c * P:(c + 1) * P], ident),
                      "pe_tg" if c == 3 else None)
        xg_free[s] = (t,)
        act.wait(t, xT_free.get(place[s]))
        hi = act.do(lambda g: g.activation(xTh[place[s]][:, :], PS[PS_X][:, :], ACT.Copy), "act_xT")
        xT_ready[s] = (hi, t)

    def x_low(s):
        hi, t = xT_ready[s]
        dve.wait(t, hi, xT_free.get(place[s]))
        lo = dve.do(lambda g: g.tensor_tensor(xTl[place[s]][:, :], PS[PS_X][:, :], f32(xTh[place[s]][:, :]),
                                              ALU.subtract), "dve_xT")
        ps_free[PS_X] = (hi, lo)
        xT_ready[s] = (hi, lo)

    def wset(n):
        j = jobs[n]
        return j[2] if j[0] == "s" else 2 + j[1]

    def up(n):
        s, w = src_no[n], wset(n)
        wh, wl = dest(w)
        bg, bu = 2 + 2 * (n % 2), 3 + 2 * (n % 2)
        pe.wait(*xT_ready[s], *ps_free[bg], *ps_free[bu], *set_ready[w, "G"], *set_ready[w, "U"])
        h, l = xTh[place[s]], xTl[place[s]]
        k = 0
        for c in range(4):
            for a, w_ in ((h, wh), (h, wl), (l, wh)):
                for bank, o in ((bg, 0), (bu, GU)):
                    k += 1
                    t = pe.do(lambda g, a=a, w_=w_, c=c, bank=bank, o=o, k=k: g.matmul(
                        PS[bank][:, 0:F], a[:, c * P:(c + 1) * P], w_[:, o + c * F:o + (c + 1) * F],
                        start=(k <= 2), stop=(k > 22)), "pe_gu" if k == 24 else None)
        gu_done[n] = t
        if last_use[s] == n:
            xT_free[place[s]] = t
        for u in "GU":
            set_freed[w, u] = (t,)

    def silu(n):
        bg = 2 + 2 * (n % 2)
        act.wait(gu_done[n], h_ready.get(n - 1))
        t = act.do(lambda g: g.activation(sg_[0][:, :], PS[bg][:, 0:F], ACT.Silu), "act_si")
        return t

    def gate(n, si):
        bg, bu = 2 + 2 * (n % 2), 3 + 2 * (n % 2)
        dve.wait(gu_done[n], si, h_T.get(n - 1))
        t = dve.do(lambda g: g.tensor_tensor(hg[0][:, 0:F], PS[bu][:, 0:F], sg_[0][:, :], ALU.mult), "dve_hg")
        h_ready[n] = t
        ps_free[bg] = (t,)
        ps_free[bu] = (t,)

    def h_transposes(n):
        pe.wait(h_ready[n], hg_pad, *ps_free[PS_H])
        for c in range(3):
            t = pe.do(lambda g, c=c: g.transpose(PS[PS_H][:, c * P:(c + 1) * P], hg[0][:, c * P:(c + 1) * P], ident),
                      "pe_th" if c == 2 else None)
        h_T[n] = t

    def h_high(n):
        act.wait(h_T[n], d_done.get(n - 1))
        return act.do(lambda g: g.activation(hTh[0][:, :], PS[PS_H][:, 0:384], ACT.Copy), "act_hT")

    def h_low(n, hi):
        dve.wait(h_T[n], hi, d_done.get(n - 1))
        lo = dve.do(lambda g: g.tensor_tensor(hTl[0][:, :], PS[PS_H][:, 0:384], f32(hTh[0][:, :]),
                                              ALU.subtract), "dve_hT")
        ps_free[PS_H] = (hi, lo)
        hT_ready[n] = (hi, lo)

    def down(n):
        w, s = wset(n), src_no[n]
        wh, wl = dest(w)
        bank = dbank[s]
        first = jobs[n][0] == "e" or jobs[n][2] == 0
        final = jobs[n][0] == "e" or jobs[n][2] == 1
        pe.wait(*hT_ready[n], *set_ready[w, "D"])
        if first:
            pe.wait(*ps_free[bank])
        k = 0
        for c in range(3):
            m = FKS[c]
            o = 2 * GU + c * H
            for a, w_ in ((hTh[0], wh), (hTh[0], wl), (hTl[0], wh)):
                k += 1
                t = pe.do(lambda g, a=a, w_=w_, c=c, m=m, o=o, k=k: g.matmul(
                    PS[bank][:, :], a[0:m, c * P:(c + 1) * P], w_[0:m, o:o + H],
                    start=(k == 1 and first), stop=(k == 9 and final)), "pe_dn" if k == 9 else None)
        d_done[n] = t
        set_freed[w, "D"] = (t,)

    def scale_out(n):
        if not (jobs[n][0] == "e" or jobs[n][2] == 1):
            return
        s = src_no[n]
        i = ob_n[0]
        ob_n[0] += 1
        wcol = XG[s % NXG][:, H + jobs[n][1]:H + jobs[n][1] + 1] if jobs[n][0] == "e" else tgf
        act.wait(d_done[n], acc_tok.get(i - 2), xg_ready[s])
        t = act.do(lambda g: g.activation(ob[i % 2][:, :], PS[dbank[s]][:, :], ACT.Copy, scale=wcol), "act_ob")
        ps_free[dbank[s]] = (t,)
        if jobs[n][0] == "e":
            xg_free[s] = (*xg_free[s], t)
        ob_ready[n] = (i, t)

    def accumulate(n):
        if n not in ob_ready:
            return
        i, t = ob_ready[n]
        pool.wait(t, acc_chain[0], stored[B - 2], stored[B - 1], ystore)
        if jobs[n][0] == "e":
            e = jobs[n][1]
            tok = pool.do(lambda g: g.indirect_dma_start(
                out=y[:, :], out_offset=bass.IndirectOffsetOnAxis(ap=idx[:, e:e + 1], axis=0),
                in_=ob[i % 2][:, :], in_offset=None, compute_op=ALU.add), "acc", 16)
        else:
            k = jobs[n][1]
            tok = dma(pool, y[k * P:(k + 1) * P, :], ob[i % 2][:, :], "acc", accum_op=ALU.add)
        acc_chain[0] = tok
        acc_tok[i] = tok

    ahead = [(e, u) for e in range(E) for u in ("G", "U", "D")]
    ahead.sort(key=lambda k: (job_of[k[0]] - (0 if k[1] == "D" else 1), k[0]))
    per_step = QUOTA * E / (NJ - lead)

    def may(e, u, n):
        if e < 2:
            return n >= lead - 4 if e == 0 else n >= lead - 1
        return job_of[e - 2] + (1 if u == "D" else 0) <= n - 1

    def must(e, u, n):
        return n >= job_of[e] - (0 if u == "D" else 1)

    gathered = [0]

    def gather_to(n):
        while gathered[0] < len(srcs) and first_use[gathered[0]] <= n + 2:
            s = gathered[0]
            if srcs[s][0] == "e" and idx_ready[0] is None:
                return
            if s >= NXG and pending(s - NXG):
                return
            gather(s)
            gathered[0] += 1

    def pending(s):
        return last_use[s] not in ob_ready if srcs[s][0] == "e" else s not in xg_free

    gather_to(0)
    x_transposes(0)
    x_low(0)
    done_units = 0
    for n in range(NJ + 1):
        todo = []
        while ahead and n < NJ:
            e, u = ahead[0]
            if not may(e, u, n):
                assert not must(e, u, n), (e, u, n)
                break
            if not must(e, u, n) and done_units >= per_step * (n - lead + SLACK):
                break
            todo.append(ahead.pop(0))
            done_units += 1
        hi_h = h_high(n - 1) if n >= 1 else None
        if n >= 1:
            h_low(n - 1, hi_h)
        if n < NJ:
            up(n)

        def split(k):
            e, u = k
            if n < lead and e == 0:
                hi = split_high(pool, 2 + e, u, "pool_wh")
                split_low(pool, 2 + e, u, hi, "pool_wl")
            else:
                if e == 1:
                    for q in (act, dve):
                        q.wait(idx_ready[0])
                hi = split_high(act, 2 + e, u, "act_wh")
                split_low(dve, 2 + e, u, hi, "dve_wl")
            if e + 2 < E:
                load_raw(2 + e + 2, u)

        room = ROOM
        while rounds and (room > 0 or n == lead - 2):
            cost, go = rounds.pop(0)
            go()
            room -= cost
        if not rounds and idx_ready[0] is None:
            finish_lists()
        half = (len(todo) * 2 + 2) // 3
        for k in todo[:half]:
            split(k)
        if n < NJ:
            si = silu(n)
            gate(n, si)
        if n + 1 < NJ and first_use[src_no[n + 1]] == n + 1:
            gather_to(n)
            x_transposes(src_no[n + 1])
            x_low(src_no[n + 1])
        if n >= 1:
            down(n - 1)
        if n < NJ:
            h_transposes(n)
        for k in todo[half:]:
            split(k)
        if n >= 1:
            scale_out(n - 1)
        gather_to(n)
        if n >= 1:
            accumulate(n - 1)
    pool.wait(acc_chain[0])

    with nc.Block() as block:
        @block.sync
        def _(g):
            sp.replay(g)

        @block.scalar
        def _(g):
            act.replay(g)

        @block.tensor
        def _(g):
            pe.replay(g)

        @block.vector
        def _(g):
            dve.replay(g)

        @block.gpsimd
        def _(g):
            pool.replay(g)
    ctx.close()


def kernel(x, ctx_1024, g_xattn, g_ffn, L0_xattn_Wq, L0_xattn_bq, L0_xattn_Wk, L0_xattn_bk, L0_ffn_gate_w,
           L0_ffn_w_gate, L0_ffn_w_up, L0_ffn_w_down, L0_ffn_sh_gate, L0_ffn_sh_up, L0_ffn_sh_down):
    import numpy as np
    import concourse.bacc as bacc
    from concourse import mybir as mb
    from concourse.bass_utils import run_bass_kernel_spmd

    nc = bacc.Bacc("TRN2", target_bir_lowering=False, num_devices=1)
    cst = np.zeros((P, 145), np.float32)
    cst[:, 0:128] = np.eye(P, dtype=np.float32)
    for t in range(NT):
        cst[:, 128 + t] = T - (P * t + np.arange(P))
    cst[:, 144] = np.arange(P)
    c = np.ascontiguousarray
    arrays = {
        "x": c(x), "ctxt": c(np.transpose(np.asarray(ctx_1024), (0, 2, 1))),
        "gx": c(np.asarray(g_xattn).reshape(1, 1)), "gf": c(np.asarray(g_ffn).reshape(1, 1)),
        "wq": c(np.asarray(L0_xattn_Wq).T), "bq": c(np.asarray(L0_xattn_bq).reshape(D, 1)),
        "wk": c(np.asarray(L0_xattn_Wk).T), "bk": c(np.asarray(L0_xattn_bk).reshape(D, 1)),
        "gw": c(np.asarray(L0_ffn_gate_w).T), "wg": c(L0_ffn_w_gate), "wu": c(L0_ffn_w_up), "wd": c(L0_ffn_w_down),
        "sg": c(np.asarray(L0_ffn_sh_gate).T), "su": c(np.asarray(L0_ffn_sh_up).T),
        "sd": c(np.asarray(L0_ffn_sh_down).T), "cst": cst,
    }
    args = [nc.dram_tensor(f"i_{n}", a.shape, mb.dt.from_np(a.dtype), kind="ExternalInput").ap()
            for n, a in arrays.items()]
    y = nc.dram_tensor("o_y", (ROWS, H), FP, kind="ExternalOutput").ap()
    rows = nc.dram_tensor("rows", (ROWS, ROW), FP, kind="Internal").ap()
    build(nc, *args, y, rows)
    r = run_bass_kernel_spmd(nc, [{f"i_{n}": a for n, a in arrays.items()}], core_ids=[0])
    return r.results[0]["o_y"][0:T].reshape(B, L, H)
```

```python
import concourse.bass as bass
from concourse import mybir
from contextlib import ExitStack

P = 128
B, L, H, C, D = 4, 512, 512, 256, 128
T = B * L
E, F, TOPK, CAP = 64, 352, 6, 128
NT = T // P
NTB = L // P
FSH = 2 * F
ROW = H + E
GU = 4 * F
WALL = 2 * GU + 3 * H
ROWS = T + P
EPS = 1e-5

FP = mybir.dt.float32
FR = mybir.dt.float32r
I32 = mybir.dt.int32
ALU = mybir.AluOpType
ACT = mybir.ActivationFunctionType
AX = mybir.AxisListType
BF = mybir.dt.bfloat16
SLOTS = E * CAP
ENTRY = 16
NPOS = 4
RING = 6
FOUND = -2.0e38
ABSENT = 3.0e38

FKS = [128, 128, F - 256]


LEAD = 4
LISTS = 3
SLACK = 4


def plan_jobs():
    halves = [("s", t, h) for t in range(NT) for h in range(2)]
    jobs, rest = halves[:2 * LEAD], halves[2 * LEAD:]
    n = len(rest)
    for e in range(E):
        jobs.append(("e", e, 0))
        if rest and (e + 1) * n // (E - 3) > n - len(rest):
            jobs.append(rest.pop(0))
    assert not rest
    return jobs, 2 * LEAD


class Queue:

    def __init__(self, book):
        self.book, self.steps, self.seen = book, [], {}

    def wait(self, *toks):
        for tok in toks:
            if tok is None:
                continue
            name, val = tok
            if self.seen.get(name, 0) < val:
                self.seen[name] = val
                sem = self.book.sem(name)
                self.steps.append(lambda eng, s=sem, v=val: eng.wait_ge(s, v))

    def do(self, fn, tag=None, by=1):
        if tag is None:
            self.steps.append(fn)
            return None
        tok = self.book.tick(tag, by)
        sem = self.book.sem(tag)
        self.steps.append(lambda eng: fn(eng).then_inc(sem, by))
        return tok

    def replay(self, eng):
        for s in self.steps:
            s(eng)


class Book:

    def __init__(self, nc, ctx):
        self.nc, self.ctx, self.sems, self.count = nc, ctx, {}, {}

    def sem(self, name):
        if name not in self.sems:
            self.sems[name] = self.ctx.enter_context(self.nc.semaphore(name))
        return self.sems[name]

    def tick(self, name, by):
        self.count[name] = self.count.get(name, 0) + by
        return (name, self.count[name])


def build(nc, x, ctxt, gx, gf, wq, bq, wk, bk, gw, wg, wu, wd, sg, su, sd, cst, tab0, y, rows, table):
    ctx = ExitStack()
    book = Book(nc, ctx)
    sp, act, pe, dve, pool = (Queue(book) for _ in range(5))

    def sb(stack, name, shape, dt=FP):
        return stack.enter_context(nc.sbuf_tensor(name, shape, dt))

    jobs, lead = plan_jobs()
    NJ = len(jobs)

    ident = sb(ctx, "ident", [P, P])[:, :]
    SWH = [sb(ctx, f"SWH{s}", [P, WALL], FR) for s in range(2)]
    SWL = [sb(ctx, f"SWL{s}", [P, WALL], FR) for s in range(2)]
    RW = [sb(ctx, f"RW{s}", [P, WALL]) for s in range(2)]
    idx = sb(ctx, "idx", [P, E], I32)
    tg2 = sb(ctx, "tg2", [P, 4])
    tgx, tgf = tg2[:, 2:3], tg2[:, 3:4]

    PS = [ctx.enter_context(nc.psum_tensor(f"PS{i}", [P, 512], FP)) for i in range(8)]

    XG3 = sb(ctx, "XG3", [P, ROW])
    actx = ExitStack()
    xs0 = sb(actx, "xs0", [P, NTB, H])
    cxs = [sb(actx, f"cx{i}", [P, 2, L]) for i in range(2)]
    wqs = sb(actx, "wqs", [P, 2, D])
    wks = sb(actx, "wks", [P, 2, D])
    QT = sb(actx, "QT", [P, L])
    KT = sb(actx, "KT", [P, L])
    At = sb(actx, "At", [P, NTB, L])
    lTh = sb(actx, "lTh", [P, 4, L], FR)
    lTl = sb(actx, "lTl", [P, 4, L], FR)
    ATh = sb(actx, "ATh", [P, 4, L], FR)
    ATl = sb(actx, "ATl", [P, 4, L], FR)
    xs = [xs0, sb(actx, "xs1", [P, NTB, H])]
    bqk = sb(actx, "bqk", [P, 2])
    gws = sb(actx, "gws", [P, 4, E])
    l2T = sb(actx, "l2T", [P, 2, 4, P])
    r2 = sb(actx, "r2", [P, RING, ROW])
    st = sb(actx, "st", [P, 2, NTB, 6])
    mv = sb(actx, "mv", [P, 2, NTB, 2])
    rs = sb(actx, "rs", [P, 2, 5, NTB])
    sm = sb(actx, "sm", [P, 3, NTB])
    cs = sb(actx, "cs", [P, P + E + NT * ENTRY])
    base, tokc = cs[:, P:P + E], cs[:, P + E:].rearrange("p (t k) -> p t k", k=ENTRY)
    tri = sb(actx, "tri", [P, P], BF)
    ones = sb(actx, "ones", [P, P], BF)
    v8 = sb(actx, "v8", [P, 2, 8])
    mr = sb(actx, "mr", [P, 2, E])
    rt = sb(actx, "rt", [P, 4, 4])
    mk = sb(actx, "mk", [P, 2, E], BF)
    run = sb(actx, "run", [P, 4, E], BF)
    key = sb(actx, "key", [P, 3, E])
    k8 = sb(actx, "k8", [P, 8])
    di = sb(actx, "di", [P, NPOS, 8], I32)
    lnx = sb(actx, "lnx", [P, NTB, H])
    tabs = lnx[0:E, :, :].rearrange("e a (s k) -> e (a s) k", k=ENTRY)
    actx.close()

    WH, WL = [None, None], [None, None]
    NXG = 4
    XG = [sb(ctx, f"XG{i}", [P, ROW]) if i < 3 else XG3 for i in range(NXG)]
    xTh = [sb(ctx, f"xTh{i}", [P, 512], FR) for i in range(3)]
    xTl = [sb(ctx, f"xTl{i}", [P, 512], FR) for i in range(3)]
    sg_ = [sb(ctx, f"sgl{i}", [P, F]) for i in range(1)]
    hg = [sb(ctx, f"hg{i}", [P, 384]) for i in range(1)]
    hTh = [sb(ctx, f"hTh{i}", [P, 384], FR) for i in range(1)]
    hTl = [sb(ctx, f"hTl{i}", [P, 384], FR) for i in range(1)]
    ob = [sb(ctx, f"ob{i}", [P, H]) for i in range(2)]
    for i in range(2):
        WH[i], WL[i] = sb(ctx, f"WH{i}", [P, WALL], FR), sb(ctx, f"WL{i}", [P, WALL], FR)

    f32 = lambda ap: ap.bitcast(FP)
    dma = lambda q, out, in_, tag, **kw: q.do(lambda g: g.dma_start(out, in_, **kw), tag, 16)

    def load_x(b):
        sp.wait(x_free.get(b - 2), stored.get(b - 2))
        x_in[b] = dma(sp, xs[b % 2][:, :, :], x[b].rearrange("(i p) n -> p i n", p=P), f"in_x{b % 2}")

    def load_ctx(b):
        sp.wait(ctx_free.get(b - 2))
        c_in[b] = dma(sp, cxs[b % 2][:, :, :], ctxt[b].rearrange("(k p) n -> p k n", p=P), f"in_ctx{b % 2}")

    x_in, c_in, x_free, ctx_free, stored = {}, {}, {}, {}, {}
    load_x(0)
    load_ctx(0)
    for o, i in ((wqs, wq), (wks, wk)):
        w_in = dma(sp, o[:, :, :], i.rearrange("(k p) d -> p k d", p=P), "in_w")
    w_in = dma(sp, bqk[:, 0:1], bq, "in_w")
    w_in = dma(sp, bqk[:, 1:2], bk, "in_w")
    cst_in = dma(act, ident, cst[:, 0:P], "in_cst")
    cst_in = dma(act, cs[:, :], cst[:, P:], "in_cst")
    table0 = dma(act, table, tab0, "in_tab")
    g_in = dma(act, tg2[:, 0:1], gx.to_broadcast([P, 1]), "in_g")
    g_in = dma(act, tg2[:, 1:2], gf.to_broadcast([P, 1]), "in_g")
    gw_in = dma(act, gws[:, :, :], gw.rearrange("(p k) e -> p k e", k=4), "in_gw")
    raw_in, raw_free = {}, {}

    def unit(u):
        return slice({"G": 0, "U": GU, "D": 2 * GU}[u], {"G": GU, "U": 2 * GU, "D": WALL}[u])

    def load_raw(n, u):
        t = RW[n % 2]
        sp.wait(*raw_free.get((n - 2, u), ()))
        if n < 2:
            cols = slice(n * F, (n + 1) * F)
            g_, u_, d_ = sg[:, cols], su[:, cols], sd[n * F:(n + 1) * F, :]
        else:
            g_, u_, d_ = wg[n - 2], wu[n - 2], wd[n - 2]
        tag = f"raw{u}{n % 2}"
        if u in "GU":
            src = (g_ if u == "G" else u_).rearrange("(p k) f -> p k f", k=4)
            tok = dma(sp, t[:, unit(u)].rearrange("p (k f) -> p k f", k=4), src, tag)
        else:
            o = 2 * GU
            dma(sp, t[:, o:o + 2 * H].rearrange("p (k n) -> p k n", k=2),
                d_[0:256, :].rearrange("(k p) n -> p k n", p=P), tag)
            tok = dma(sp, t[0:FKS[2], o + 2 * H:o + 3 * H], d_[256:F, :], tag)
        raw_in[n, u] = tok

    load_raw(0, "G")
    load_x(1)

    set_ready, set_freed = {}, {}

    def pieces(u):
        if u in "GU":
            s = unit(u)
            return [(P, s.start, s.stop)]
        o = 2 * GU
        return [(P, o, o + 2 * H), (FKS[2], o + 2 * H, o + 3 * H)]

    def dest(n):
        return (SWH[n], SWL[n]) if n < 2 else (WH[n % 2], WL[n % 2])

    def split_high(q, n, u, what):
        h, _ = dest(n)
        q.wait(raw_in[n, u], *set_freed.get((n - 2, u), ()))
        for np_, a, b in pieces(u):
            if q is act:
                fn = lambda g, np_=np_, a=a, b=b: g.activation(h[0:np_, a:b], RW[n % 2][0:np_, a:b], ACT.Copy)
            else:
                fn = lambda g, np_=np_, a=a, b=b: g.tensor_copy(h[0:np_, a:b], RW[n % 2][0:np_, a:b])
            tok = q.do(fn, what)
        return tok

    def split_low(q, n, u, high, what):
        h, l = dest(n)
        toks = []
        for k, (np_, a, b) in enumerate(pieces(u)):
            r, w = (pool, "pool_wl") if k and n > 3 else (q, what)
            r.wait(raw_in[n, u], *set_freed.get((n - 2, u), ()), high)
            tok = r.do(lambda g, np_=np_, a=a, b=b: g.tensor_tensor(
                l[0:np_, a:b], RW[n % 2][0:np_, a:b], f32(h[0:np_, a:b]), ALU.subtract), w)
            toks.append(tok)
        raw_free[n, u] = tuple(toks)
        set_ready[n, u] = (high, *toks)

    shared_units = [(n, u) for n in range(2) for u in "GUD"]

    shared_high = {}

    def split_shared(hi, lo):
        while hi > len(shared_high) and len(shared_high) < 6:
            n, u = shared_units[len(shared_high)]
            shared_high[n, u] = split_high(act, n, u, "act_wh")
        for n, u in shared_units[len(early_done):lo]:
            split_low(pool, n, u, shared_high[n, u], "pool_wl")
            early.append((2 + n, u))
            early_done.append(1)

    early_done = []
    early = []

    def load_early():
        while early:
            load_raw(*early.pop(0))

    act.wait(g_in)
    tg_ready = act.do(lambda g: g.activation(tg2[:, 2:4], tg2[:, 0:2], ACT.Tanh), "act_tg")
    z = dve.do(lambda g: g.memset(At[:, 0:2, :], 0.0), "dve_z")
    sp.wait(z)
    zero = dma(sp, y[T:ROWS, :], At[:, 0, :], "out_z")
    zero = dma(sp, rows[T:ROWS, 0:H], At[:, 0, :], "out_z")
    zero = dma(sp, rows[T:ROWS, H:ROW], At[:, 1, 0:E], "out_z")
    dve.do(lambda g: g.memset(ones[:, :], 1.0), "dve_c")
    dve.do(lambda g: g.memset(run[:, 0, :], 0.0), "dve_c")
    dve.wait(cst_in)
    tri_ready = dve.do(lambda g: g.tensor_copy(tri[:, :], cs[:, 0:P]), "dve_c")
    nh = pool.do(lambda g: g.memset(rs[:, 0, 3, :], -0.5), "pool_nh")
    nh = pool.do(lambda g: g.memset(rs[:, 1, 3, :], -0.5), "pool_nh")

    ps_free = [() for _ in range(8)]

    mv_done = {}

    def bn(w, src, i):
        return dve.do(lambda g: g.bn_stats(st[:, w, i, :], src[:, i, :]), "dve_st")

    def rstd(w, s, q):
        dve.wait(s)
        for i in range(NTB):
            s = dve.do(lambda g, i=i: g.bn_aggr(mv[:, w, i, :], st[:, w, i, :]), "dve_mv")
        mv_done[w] = s
        ve, r, t = (rs[:, w, k, :] for k in range(3))
        if q is not dve:
            pool.wait(s, nh)
            s = pool.do(lambda g: g.tensor_scalar(ve, mv[:, w, :, 1], EPS, None, ALU.add), "pool_rs")
            pool.wait(s)
            s = pool.do(lambda g: g.tensor_tensor(r, ve, rs[:, w, 3, :], ALU.pow), "pool_rs")
            pool.wait(s)
            s = pool.do(lambda g: g.tensor_tensor(t, r, r, ALU.mult), "pool_rs")
            pool.wait(s)
            s = pool.do(lambda g: g.tensor_tensor(t, t, ve, ALU.mult), "pool_rs")
            pool.wait(s)
            s = pool.do(lambda g: g.tensor_scalar(t, t, -0.5, 1.5, ALU.mult, ALU.add), "pool_rs")
            pool.wait(s)
            s = pool.do(lambda g: g.tensor_tensor(r, r, t, ALU.mult), "pool_rs")
            pool.wait(s)
            s = pool.do(lambda g: g.tensor_tensor(t, mv[:, w, :, 0], r, ALU.mult), "pool_rs")
            pool.wait(s)
            s = pool.do(lambda g: g.tensor_scalar(rs[:, w, 4, :], t, -1.0, None, ALU.mult), "pool_rs")
            return s
        def step(fn):
            dve.wait(step.tok)
            step.tok = dve.do(fn, "dve_rs")
        step.tok = s
        step(lambda g: g.tensor_scalar(ve, mv[:, w, :, 1], EPS, None, ALU.add))
        step(lambda g: g.tensor_scalar(t.bitcast(I32), ve.bitcast(I32), 1, None, ALU.logical_shift_right))
        step(lambda g: g.tensor_scalar(r.bitcast(I32), t.bitcast(I32), -1.0, float(0x5F3759DF), ALU.mult, ALU.add))
        for _ in range(3):
            step(lambda g: g.scalar_tensor_tensor(out=t, in0=r, scalar=-0.5, in1=r, op0=ALU.mult, op1=ALU.mult))
            step(lambda g: g.tensor_tensor(t, t, ve, ALU.mult))
            step(lambda g: g.scalar_tensor_tensor(out=r, in0=t, scalar=1.5, in1=r, op0=ALU.add, op1=ALU.mult))
        step(lambda g: g.scalar_tensor_tensor(out=rs[:, w, 4, :], in0=mv[:, w, :, 0], scalar=-1.0, in1=r,
                                              op0=ALU.mult, op1=ALU.mult))
        return step.tok

    ln_free, ln_done, ln_read = {}, {}, {}

    rs1 = {}

    def stats1(b):
        dve.wait(x_in[b], mv_done.get(0), rs1.get(b - 1))
        for i in range(NTB):
            s = bn(0, xs[b % 2], i)
        pool.wait(ln_done.get((b - 1, NTB - 1)))
        rs1[b] = rstd(0, s, pool)

    def apply1(b):
        for i in range(NTB):
            act.wait(rs1[b], ln_read.get((b - 1, i)), x_in[b])
            ln_done[b, i] = act.do(lambda g, i=i: g.activation(
                lnx[:, i, :], xs[b % 2][:, i, :], ACT.Identity, bias=rs[:, 0, 4, i:i + 1],
                scale=rs[:, 0, 1, i:i + 1]), "act_ln")

    lT_ready, xm_done = {}, {}

    def transpose_ln(b, i):
        k = 0
        pe.wait(ln_done[b, i], cst_in, *ps_free[k])
        for c in range(4):
            s = pe.do(lambda g, c=c: g.transpose(PS[k][:, c * P:(c + 1) * P], lnx[:, i, c * P:(c + 1) * P], ident),
                      "pe_tx" if c == 3 else None)
        act.wait(s, xm_done.get((b - 1, i)))
        src = PS[k][:, :].rearrange("p (c m) -> p c m", c=4)
        hi = act.do(lambda g: g.activation(lTh[:, :, i * P:(i + 1) * P], src, ACT.Copy), "act_lT")
        dve.wait(s, hi, xm_done.get((b - 1, i)))
        lo = dve.do(lambda g: g.tensor_tensor(
            lTl[:, :, i * P:(i + 1) * P], src, f32(lTh[:, :, i * P:(i + 1) * P]), ALU.subtract), "dve_lT")
        ps_free[k] = (hi, lo)
        ln_free[b] = ln_read[b, i] = s
        lT_ready[b, i] = (hi, lo)

    qk_ready, en_done, at_ready, at_free, AT_ready = {}, {}, {}, {}, {}

    def project(b, which=(0, 1)):
        pe.wait(c_in[b], w_in)
        for k in which:
            w, o = ((wqs, QT), (wks, KT))[k]
            bank = 6 + k
            pe.wait(*ps_free[bank])
            for c in range(2):
                s = pe.do(lambda g, w=w, c=c, bank=bank: g.matmul(PS[bank][:, :], w[:, c, :], cxs[b % 2][:, c, :],
                                                                  start=(c == 0), stop=(c == 1)),
                          "pe_pj" if c == 1 else None)
            act.wait(s, w_in, en_done.get(b - 1))
            t = act.do(lambda g, k=k, o=o, bank=bank: g.activation(o[:, :], PS[bank][:, :], ACT.Identity,
                                                                   bias=bqk[:, k:k + 1]), "act_qk")
            ps_free[bank] = (t,)
        ctx_free[b] = s
        qk_ready[b] = t

    exp_done = {}

    def inverse(b, m):
        dve.wait(exp_done[b, m])
        inv[b, m] = dve.do(lambda g: g.reciprocal(sm[:, 2, m:m + 1], sm[:, 1, m:m + 1]), "dve_rc")

    def normalise(b, m):
        act.wait(inv[b, m])
        at_ready[b, m] = act.do(lambda g: g.activation(At[:, m, :], At[:, m, :], ACT.Copy,
                                                       scale=sm[:, 2, m:m + 1]), "act_at")

    inv, top = {}, {}

    def energy(b, m):
        pe.wait(qk_ready[b])
        bank = 2 + m % 2
        pe.wait(*ps_free[bank])
        s = pe.do(lambda g: g.matmul(PS[bank][:, :], QT[:, m * P:(m + 1) * P], KT[:, :], start=True, stop=True),
                  "pe_en")
        en_done[b] = s
        scored[b, m] = s

    scored = {}

    def maximum(b, m):
        dve.wait(scored[b, m])
        top[b, m] = dve.do(lambda g: g.tensor_reduce(sm[:, 0, m:m + 1], PS[2 + m % 2][:, :], AX.X, ALU.max,
                                                     negate=True), "dve_mx")

    def exponent(b, m):
        act.wait(scored[b, m], top[b, m], at_free.get(b - 1), zero)
        a = act.do(lambda g: g.activation(At[:, m, :], PS[2 + m % 2][:, :], ACT.Exp, bias=sm[:, 0, m:m + 1],
                                          accum_out=sm[:, 1, m:m + 1]), "act_ex")
        ps_free[2 + m % 2] = (a,)
        exp_done[b, m] = a

    def transpose_at(b, tiles=range(NTB)):
        for m in tiles:
            k = (0, 4, 1, 5)[m]
            pe.wait(at_ready[b, m], *ps_free[k])
            for c in range(4):
                fn = lambda g, m=m, c=c, k=k: g.transpose(PS[k][:, c * P:(c + 1) * P],
                                                          At[:, m, c * P:(c + 1) * P], ident)
                s = pe.do(fn, "pe_ta" if c == 3 else None)
            src = PS[k][:, :].rearrange("p (c m) -> p c m", c=4)
            act.wait(s, xm_done.get((b - 1, NTB - 1)))
            hi = act.do(lambda g, m=m, src=src: g.activation(ATh[:, :, m * P:(m + 1) * P], src, ACT.Copy), "act_AT")
            dve.wait(s, hi)
            lo = dve.do(lambda g, m=m, src=src: g.tensor_tensor(
                ATl[:, :, m * P:(m + 1) * P], src, f32(ATh[:, :, m * P:(m + 1) * P]), ALU.subtract), "dve_AT")
            ps_free[k] = (hi, lo)
        at_free[b] = s
        AT_ready[b] = (hi, lo)

    x2_ready = {}

    steps = [[], [], []]

    def follow_up():
        new, old, oldest = ({k: v for k, *v in s} for s in steps)
        if "e" in old:
            inverse(*old["e"])
        if "r" in new:
            route_copy(*new["r"])
        if "e" in new:
            maximum(*new["e"])
        if "e" in old:
            normalise(*old["e"])
        if "e" in new:
            exponent(*new["e"])
        if "r" in new:
            route_top(*new["r"])
            route_mark(*new["r"])
        if "r" in old:
            route_slots(*old["r"])
            if old["r"][0] < B - 1:
                score(*old["r"])
        if "r" in oldest:
            if oldest["r"][0] < B - 1:
                score_row(*oldest["r"])
        steps.insert(0, [])
        steps.pop()

    def mix(b, also={}):
        xb = xs[b % 2]
        for i in range(NTB):
            if i + 1 < NTB:
                transpose_ln(b, i + 1)
            follow_up()
            send_slots()
            if (i, "pre") in also:
                also[i, "pre"]()
            if b == B - 1 and i:
                route_transpose(b - 1, i)
            bank = 4 + i % 2
            pe.wait(*AT_ready[b], *lT_ready[b, i], *ps_free[bank])
            n = 0
            for c in range(4):
                for a, w in ((lTh, ATh), (lTh, ATl), (lTl, ATh)):
                    s = pe.do(lambda g, i=i, c=c, a=a, w=w, bank=bank, n=n: g.matmul(
                        PS[bank][:, :], a[:, c, i * P:(i + 1) * P], w[:, c, :], start=(n == 0), stop=(n == 11)),
                        "pe_xm" if n == 11 else None)
                    n += 1
            xm_done[b, i] = s
            if b and not (b == B - 1 and i):
                route_transpose(b - 1, i)
            if b + 1 < B:
                energy(b + 1, i)
                steps[0].append(("e", b + 1, i))
            if b:
                route_logits(b - 1, i)
                steps[0].append(("r", b - 1, i))
            dve.wait(s, tg_ready)
            t = dve.do(lambda g, i=i, bank=bank: g.scalar_tensor_tensor(
                out=xb[:, i, :], in0=PS[bank][:, :], scalar=tgx, in1=xb[:, i, :], op0=ALU.mult, op1=ALU.add),
                "dve_x2")
            ps_free[bank] = (t,)
            dve.wait(t)
            x2_ready[b] = bn(1, xb, i)
            if (i, "post") in also:
                also[i, "post"]()
            if i in also:
                also[i]()
        sp.wait(t)
        stored[b] = dma(sp, y[b * L:(b + 1) * L, :].rearrange("(i p) n -> p i n", p=P), xb[:, :, :], f"out_x{b % 2}")

    rowst, l2_ready, lg_done, t2_done, score_done, tops = {}, {}, {}, {}, {}, {}

    def layer2(b, tiles=range(NTB)):
        act.wait(rs2[b])
        for i in tiles:
            tile = b * NTB + i
            assert tile < RING or tile - RING in rowst
            act.wait(rowst.get(tile - RING), t2_done.get(tile - RING), x2_ready[b])
            s = act.do(lambda g, i=i, tile=tile: g.activation(
                r2[:, tile % RING, 0:H].rearrange("p (k m) -> p k m", k=4),
                xs[b % 2][:, i, :].rearrange("p (m k) -> p k m", k=4), ACT.Identity,
                bias=rs[:, 1, 4, i:i + 1], scale=rs[:, 1, 1, i:i + 1]), "act_n2")
            l2_ready[b, i] = s
        x_free[b] = s

    def lbank(tile):
        return 6 + tile % 2 if tile < NT - NTB else 7

    def route_transpose(b, i):
        tile = b * NTB + i
        k = 1 if b < B - 1 else i % 2
        pe.wait(l2_ready[b, i], *ps_free[k])
        for c in range(4):
            s = pe.do(lambda g, c=c: g.transpose(PS[k][:, c * P:(c + 1) * P], r2[:, tile % RING, c * P:(c + 1) * P], ident),
                      "pe_t2" if c == 3 else None)
        t2_done[tile] = s
        act.wait(s, lg_done.get(tile - 2))
        t = act.do(lambda g: g.activation(l2T[:, tile % 2, :, :], PS[k][:, :].rearrange("p (c m) -> p c m", c=4),
                                          ACT.Copy), "act_l2")
        ps_free[k] = (t,)

    def route_logits(b, i):
        tile = b * NTB + i
        bank = lbank(tile)
        pe.wait(("act_l2", book.count["act_l2"]), gw_in, *ps_free[bank])
        for c in range(4):
            s = pe.do(lambda g, c=c: g.matmul(PS[bank][:, 0:E], l2T[:, tile % 2, c, :], gws[:, c, :],
                                              start=(c == 0), stop=(c == 3)), "pe_lg" if c == 3 else None)
        lg_done[tile] = s

    def route_copy(b, i):
        tile = b * NTB + i
        act.wait(lg_done[tile], rowst.get(tile - RING))
        lg_read[tile] = act.do(lambda g: g.activation(r2[:, tile % RING, H:ROW], PS[lbank(tile)][:, 0:E], ACT.Copy), "act_lg")

    def route_top(b, i):
        tile = b * NTB + i
        j = tile % 2
        dve.wait(lg_read[tile], exp_of.get(tile - 2))
        t = dve.do(lambda g: g.max(v8[:, j, :], r2[:, tile % RING, H:ROW]), "dve_v8")
        dve.wait(t)
        n = dve.do(lambda g: g.tensor_scalar(rt[:, i, 0:1], v8[:, j, 0:1], -1.0, None, ALU.mult), "dve_nm")
        t = dve.do(lambda g: g.memset(v8[:, j, TOPK:8], ABSENT), "dve_nm")
        tops[tile] = (t, n)

    def route_mark(b, i):
        tile = b * NTB + i
        j = tile % 2
        t, n = tops[tile]
        dve.wait(t, pos_done.get(tile - 2))
        t = dve.do(lambda g: g.match_replace(mr[:, j, :], v8[:, j, :], r2[:, tile % RING, H:ROW], FOUND), "dve_mr")
        replaced[tile] = t
        dve.wait(t, run_done.get(tile - 1))
        mask_done[tile] = dve.do(lambda g: g.tensor_scalar(mk[:, j, :], mr[:, j, :], FOUND, None, ALU.is_equal), "dve_mk")
        dve.wait(mask_done[tile])
        run_done[tile] = dve.do(lambda g: g.tensor_tensor(run[:, (tile + 1) % 4, :], run[:, tile % 4, :], mk[:, j, :], ALU.add),
                                "dve_run")

    exp_of, replaced = {}, {}

    def score(b, i):
        tile = b * NTB + i
        sc = r2[:, tile % RING, H:ROW]
        act.wait(replaced[tile], tops[tile][1])
        a = act.do(lambda g: g.activation(sc, sc, ACT.Exp, bias=rt[:, i, 0:1], accum_out=rt[:, i, 1:2]), "act_sc")
        exp_of[tile] = a

    def score_row(b, i):
        tile = b * NTB + i
        sc = r2[:, tile % RING, H:ROW]
        dve.wait(exp_of[tile])
        t = dve.do(lambda g: g.reciprocal(rt[:, i, 2:3], rt[:, i, 1:2]), "dve_mr")
        dve.wait(t, tg_ready)
        t = dve.do(lambda g: g.tensor_scalar(sc, sc, rt[:, i, 2:3], tgf, ALU.mult, ALU.mult), "dve_sc")
        score_done[tile] = t
        sp.wait(t)
        rowst[tile] = dma(sp, rows[tile * P:(tile + 1) * P, :], r2[:, tile % RING, :], f"out_row{tile % RING}")

    lg_read, mask_done, run_done, pos_done, scattered = {}, {}, {}, {}, {}

    def route_slots(b, i):
        tile = b * NTB + i
        j = tile % 2
        bank = lbank(tile)
        ps = PS[bank][:, E:2 * E]
        pe.wait(mask_done[tile], lg_read[tile], run_done.get(tile - 1), tri_ready)
        pe.do(lambda g, ps=ps, j=j: g.matmul(ps, tri[:, :], mk[:, j, :], start=True, stop=False))
        s = pe.do(lambda g, ps=ps, j=j: g.matmul(ps, ones[:, :], run[:, tile % 4, :], start=False, stop=True), "pe_ps")
        ps_done[tile] = s
        dve.wait(s, pos_done.get(tile - 1))
        dve.do(lambda g, ps=ps, j=j: g.scalar_tensor_tensor(
            out=key[:, 0, :], in0=ps, scalar=CAP - 0.5, in1=mk[:, j, :], op0=ALU.is_lt, op1=ALU.mult), "dve_pk")
        t = dve.do(lambda g, ps=ps: g.tensor_tensor(key[:, 1, :], base, ps, ALU.subtract), "dve_pk")
        ps_free[bank] = (t,)
        dve.wait(t, cst_in)
        t = dve.do(lambda g: g.tensor_tensor(key[:, 2, :], key[:, 0, :], key[:, 1, :], ALU.mult), "dve_pk")
        pos_done[tile] = t
        dve.wait(t)
        t = dve.do(lambda g: g.max(k8[:, :], key[:, 2, :]), "dve_pk")
        dve.wait(t, scattered.get(tile - NPOS))
        n = tile % NPOS
        t = dve.do(lambda g, n=n: g.tensor_scalar(di[:, n, 0:TOPK], k8[:, 0:TOPK], -1.0, float(2 * SLOTS),
                                                  ALU.mult, ALU.add), "dve_di")
        pos_done[tile] = t
        unsent.append((tile, t))

    unsent = []

    def send_slots():
        while unsent:
            tile, t = unsent.pop(0)
            n = tile % NPOS
            pool.wait(t, table0, cst_in)
            for k in range(TOPK):
                scattered[tile] = pool.do(lambda g, k=k, n=n, tile=tile: g.indirect_dma_start(
                    out=table, out_offset=bass.IndirectOffsetOnAxis(ap=di[:, n, k:k + 1], axis=0),
                    in_=tokc[:, tile, :], in_offset=None, bounds_check=SLOTS - 1, oob_is_err=False),
                    f"scat{n}", 16)

    ps_done = {}

    rs2 = {}

    load_ctx(1)
    for n in range(2):
        for u in "GUD":
            if n or u != "G":
                load_raw(n, u)
    stats1(0)
    project(0)
    apply1(0)
    stats1(1)
    transpose_ln(0, 0)
    for i in range(NTB):
        energy(0, i)
        maximum(0, i)
        exponent(0, i)
    for i in range(NTB):
        inverse(0, i)
        normalise(0, i)
    transpose_at(0)
    project(1)
    split_shared(2, 1)
    for b in range(B - 1):
        if b + 2 < B:
            load_ctx(b + 2)
        also = {}
        if b:
            also[1, "post"] = lambda b=b: stats1(b + 1)
        else:
            for i in range(NTB):
                also[i, "pre"] = lambda i=i: split_shared(3 + i, 2 + i)
        mix(b, also)
        rs2[b] = rstd(1, x2_ready[b], pool)
        apply1(b + 1)
        follow_up()
        transpose_ln(b + 1, 0)
        if b + 2 < B:
            project(b + 2, (0,))
        transpose_at(b + 1, (0, 1))
        follow_up()
        transpose_at(b + 1, (2, 3))
        if b + 2 < B:
            project(b + 2, (1,))
        if b == 0:
            split_shared(6, 6)
        layer2(b)
        if b + 2 < B:
            load_x(b + 2)
        send_slots()
        load_early()
    load_early()
    last = B - 1
    tail = [lambda: (route_transpose(last, 0), route_transpose(last, 1)),
            lambda: (route_logits(last, 0), route_copy(last, 0), route_top(last, 0), route_mark(last, 0))]
    for i in range(1, NTB):
        tail.append(lambda i=i: (route_slots(last, i - 1), send_slots(), i + 1 < NTB and route_transpose(last, i + 1)))
        tail.append(lambda i=i: (route_logits(last, i), route_copy(last, i), route_top(last, i), route_mark(last, i)))
    tail.append(lambda: (route_slots(last, NTB - 1), send_slots()))

    def one_of_tail():
        if tail:
            tail.pop(0)()

    idx_ready = [None]

    def finish_lists():
        while tail:
            one_of_tail()
        bank = 7
        sp.wait(*scattered.values())
        tab_in = dma(sp, tabs, table.rearrange("(e s) k -> e s k", e=E), "in_tabs")
        for i in range(NTB):
            score(last, i)
        for i in range(NTB):
            score_row(last, i)
        pe.wait(tab_in, *ps_free[bank])
        s = pe.do(lambda g: g.transpose(PS[bank][:, 0:E], tabs[:, :, 0], ident[0:E, 0:E]), "pe_ix")
        dve.wait(s)
        idx_ready[0] = dve.do(lambda g: g.tensor_copy(idx[:, :], PS[bank][:, 0:E]), "dve_ix")
        ps_free[bank] = (idx_ready[0],)

    over_small = [at_free[B - 1], en_done[B - 1], ctx_free[B - 1], x_free[B - 2], stored[B - 2], zero]

    def over_first():
        return [xm_done[B - 1, NTB - 1], x_free[B - 1], stored[B - 1]]

    def over_second():
        return [lg_done[NT - 1], ps_done[NT - 1], score_done[NT - 1], *(rowst[NT - 1 - i] for i in range(RING)),
                gw_in, cst_in, pos_done[NT - 1], ln_free[B - 1], idx_ready[0], *scattered.values()]

    job_of = {j[1]: n for n, j in enumerate(jobs) if j[0] == "e"}
    srcs = [j for j in jobs if j[2] == 0]
    src_no = [srcs.index((j[0], j[1], 0)) for j in jobs]
    first_use = {s: src_no.index(s) for s in range(len(srcs))}
    last_use = {s: n for n, s in enumerate(src_no)}
    place = [j[1] % 2 if j[0] == "e" else (2, 0, 1)[j[1] % 3] if j[1] < LEAD else 2 for j in srcs]
    dbank = [6 if j[0] == "e" else 6 if j[1] < LEAD else 7 for j in srcs]

    xg_ready, xg_free, xT_ready, xT_free = {}, {}, {}, {}
    gu_done, h_ready, h_T, hT_ready, hT_free, d_done, ob_ready, acc_tok = {}, {}, {}, {}, {}, {}, {}, {}
    acc_chain = [None]
    ob_n = [0]
    d_free = {}

    PS_X, PS_H = 0, 1
    dve.wait(*over_small)
    hg_pad = dve.do(lambda g: g.memset(hg[0][:, F:384], 0.0), "dve_pad")

    def gather(s):
        kind, k = srcs[s][0:2]
        q = pool if kind == "e" else act
        q.wait(*xg_free.get(s - NXG, ()))
        tag = f"xg{s % NXG}" if kind == "e" else f"xh{s % NXG}"
        if kind == "e":
            pool.wait(*over_small, idx_ready[0], *(rowst[NT - 1 - i] for i in range(RING)), zero)
            xg_ready[s] = pool.do(lambda g: g.indirect_dma_start(
                out=XG[s % NXG][:, :], out_offset=None, in_=rows[:, :],
                in_offset=bass.IndirectOffsetOnAxis(ap=idx[:, k:k + 1], axis=0)), tag, 16)
        else:
            act.wait(*over_small, rowst[k])
            xg_ready[s] = dma(act, XG[s % NXG][:, :], rows[k * P:(k + 1) * P, :], tag)

    def x_transposes(s):
        before = [r for r in range(s) if place[r] == place[s]]
        assert all(last_use[r] < first_use[s] for r in before)
        pe.wait(xg_ready[s], *ps_free[PS_X])
        for c in range(4):
            t = pe.do(lambda g, c=c: g.transpose(PS[PS_X][:, c * P:(c + 1) * P],
                                                 XG[s % NXG][:, c * P:(c + 1) * P], ident),
                      "pe_tg" if c == 3 else None)
        xg_free[s] = (t,)
        act.wait(t, xT_free.get(place[s]))
        hi = act.do(lambda g: g.activation(xTh[place[s]][:, :], PS[PS_X][:, :], ACT.Copy), "act_xT")
        xT_ready[s] = (hi, t)

    def x_low(s):
        hi, t = xT_ready[s]
        dve.wait(t, hi, xT_free.get(place[s]))
        lo = dve.do(lambda g: g.tensor_tensor(xTl[place[s]][:, :], PS[PS_X][:, :], f32(xTh[place[s]][:, :]),
                                              ALU.subtract), "dve_xT")
        ps_free[PS_X] = (hi, lo)
        xT_ready[s] = (hi, lo)

    def wset(n):
        j = jobs[n]
        return j[2] if j[0] == "s" else 2 + j[1]

    def up(n):
        s, w = src_no[n], wset(n)
        wh, wl = dest(w)
        bg, bu = 2 + 2 * (n % 2), 3 + 2 * (n % 2)
        pe.wait(*xT_ready[s], *ps_free[bg], *ps_free[bu], *set_ready[w, "G"], *set_ready[w, "U"])
        h, l = xTh[place[s]], xTl[place[s]]
        k = 0
        for c in range(4):
            for a, w_ in ((h, wh), (h, wl), (l, wh)):
                for bank, o in ((bg, 0), (bu, GU)):
                    k += 1
                    t = pe.do(lambda g, a=a, w_=w_, c=c, bank=bank, o=o, k=k: g.matmul(
                        PS[bank][:, 0:F], a[:, c * P:(c + 1) * P], w_[:, o + c * F:o + (c + 1) * F],
                        start=(k <= 2), stop=(k > 22)), "pe_gu" if k == 24 else None)
        gu_done[n] = t
        if last_use[s] == n:
            xT_free[place[s]] = t
        for u in "GU":
            set_freed[w, u] = (t,)

    def silu(n):
        bg = 2 + 2 * (n % 2)
        act.wait(gu_done[n], h_ready.get(n - 1))
        t = act.do(lambda g: g.activation(sg_[0][:, :], PS[bg][:, 0:F], ACT.Silu), "act_si")
        return t

    def gate(n, si):
        bg, bu = 2 + 2 * (n % 2), 3 + 2 * (n % 2)
        dve.wait(gu_done[n], si, h_T.get(n - 1))
        t = dve.do(lambda g: g.tensor_tensor(hg[0][:, 0:F], PS[bu][:, 0:F], sg_[0][:, :], ALU.mult), "dve_hg")
        h_ready[n] = t
        ps_free[bg] = (t,)
        ps_free[bu] = (t,)

    def h_transposes(n):
        pe.wait(h_ready[n], hg_pad, *ps_free[PS_H])
        for c in range(3):
            t = pe.do(lambda g, c=c: g.transpose(PS[PS_H][:, c * P:(c + 1) * P], hg[0][:, c * P:(c + 1) * P], ident),
                      "pe_th" if c == 2 else None)
        h_T[n] = t

    def h_high(n):
        act.wait(h_T[n], d_done.get(n - 1))
        return act.do(lambda g: g.activation(hTh[0][:, :], PS[PS_H][:, 0:384], ACT.Copy), "act_hT")

    def h_low(n, hi):
        dve.wait(h_T[n], hi, d_done.get(n - 1))
        lo = dve.do(lambda g: g.tensor_tensor(hTl[0][:, :], PS[PS_H][:, 0:384], f32(hTh[0][:, :]),
                                              ALU.subtract), "dve_hT")
        ps_free[PS_H] = (hi, lo)
        hT_ready[n] = (hi, lo)

    def down(n):
        w, s = wset(n), src_no[n]
        wh, wl = dest(w)
        bank = dbank[s]
        first = jobs[n][0] == "e" or jobs[n][2] == 0
        final = jobs[n][0] == "e" or jobs[n][2] == 1
        pe.wait(*hT_ready[n], *set_ready[w, "D"])
        if first:
            pe.wait(*ps_free[bank])
        k = 0
        for c in range(3):
            m = FKS[c]
            o = 2 * GU + c * H
            for a, w_ in ((hTh[0], wh), (hTh[0], wl), (hTl[0], wh)):
                k += 1
                t = pe.do(lambda g, a=a, w_=w_, c=c, m=m, o=o, k=k: g.matmul(
                    PS[bank][:, :], a[0:m, c * P:(c + 1) * P], w_[0:m, o:o + H],
                    start=(k == 1 and first), stop=(k == 9 and final)), "pe_dn" if k == 9 else None)
        d_done[n] = t
        set_freed[w, "D"] = (t,)

    def scale_out(n):
        if not (jobs[n][0] == "e" or jobs[n][2] == 1):
            return
        s = src_no[n]
        i = ob_n[0]
        ob_n[0] += 1
        wcol = XG[s % NXG][:, H + jobs[n][1]:H + jobs[n][1] + 1] if jobs[n][0] == "e" else tgf
        act.wait(d_done[n], acc_tok.get(i - 2), xg_ready[s])
        t = act.do(lambda g: g.activation(ob[i % 2][:, :], PS[dbank[s]][:, :], ACT.Copy, scale=wcol), "act_ob")
        ps_free[dbank[s]] = (t,)
        if jobs[n][0] == "e":
            xg_free[s] = (*xg_free[s], t)
        ob_ready[n] = (i, t)

    def accumulate(n):
        if n not in ob_ready:
            return
        i, t = ob_ready[n]
        pool.wait(t, acc_chain[0], stored[B - 2], stored[B - 1], zero)
        if jobs[n][0] == "e":
            e = jobs[n][1]
            tok = pool.do(lambda g: g.indirect_dma_start(
                out=y[:, :], out_offset=bass.IndirectOffsetOnAxis(ap=idx[:, e:e + 1], axis=0),
                in_=ob[i % 2][:, :], in_offset=None, compute_op=ALU.add), "acc", 16)
        else:
            k = jobs[n][1]
            tok = dma(pool, y[k * P:(k + 1) * P, :], ob[i % 2][:, :], "acc", accum_op=ALU.add)
        acc_chain[0] = tok
        acc_tok[i] = tok

    ahead = [(e, u) for e in range(E) for u in ("G", "U", "D")]
    ahead.sort(key=lambda k: (job_of[k[0]] - (0 if k[1] == "D" else 1), k[0]))
    per_step = 3 * E / (NJ - lead)

    def may(e, u, n):
        if e < 2:
            return n >= 1 if e == 0 else idx_ready[0] is not None
        return job_of[e - 2] + (1 if u == "D" else 0) <= n - 1

    def must(e, u, n):
        return n >= job_of[e] - (0 if u == "D" else 1)

    gathered = [0]

    def gather_to(n):
        while gathered[0] < len(srcs) and first_use[gathered[0]] <= n + 3:
            s = gathered[0]
            if srcs[s][0] == "e" and idx_ready[0] is None:
                return
            if s >= NXG and pending(s - NXG):
                return
            gather(s)
            gathered[0] += 1

    def pending(s):
        return last_use[s] not in ob_ready if srcs[s][0] == "e" else s not in xg_free

    send_slots()

    def first_source():
        gather_to(0)
        x_transposes(0)
        x_low(0)

    mix(B - 1, {2: first_source})
    up(0)
    follow_up()
    rs2[B - 1] = rstd(1, x2_ready[B - 1], dve)
    layer2(B - 1, (0, 1, 2))
    follow_up()
    layer2(B - 1, (3,))
    follow_up()
    send_slots()
    done_units = 0
    for n in range(NJ + 1):
        todo = []
        while ahead and n < NJ:
            e, u = ahead[0]
            if not may(e, u, n):
                assert not must(e, u, n), (e, u, n)
                break
            if not must(e, u, n) and done_units >= per_step * (n - lead + SLACK):
                break
            todo.append(ahead.pop(0))
            done_units += 1
        hi_h = h_high(n - 1) if n >= 1 else None
        if n >= 1:
            h_low(n - 1, hi_h)
        if 0 < n < NJ:
            up(n)
        one_of_tail()

        def split(k):
            e, u = k
            if e < 2:
                for q in (act, dve):
                    q.wait(*(over_second() if e else over_first()))
            hi = split_high(act, 2 + e, u, "act_wh")
            split_low(dve, 2 + e, u, hi, "dve_wl")
            if e + 2 < E:
                load_raw(2 + e + 2, u)

        if n == lead - LISTS:
            finish_lists()
        half = (len(todo) * 2 + 2) // 3
        for k in todo[:half]:
            split(k)
        if n < NJ:
            si = silu(n)
            gate(n, si)
        if n + 1 < NJ and first_use[src_no[n + 1]] == n + 1:
            gather_to(n)
            x_transposes(src_no[n + 1])
            x_low(src_no[n + 1])
        one_of_tail()
        if n >= 1:
            down(n - 1)
        if n < NJ:
            h_transposes(n)
        one_of_tail()
        for k in todo[half:]:
            split(k)
        if n >= 1:
            scale_out(n - 1)
        gather_to(n)
        if n >= 1:
            accumulate(n - 1)
    pool.wait(acc_chain[0])

    with nc.Block() as block:
        @block.sync
        def _(g):
            sp.replay(g)

        @block.scalar
        def _(g):
            act.replay(g)

        @block.tensor
        def _(g):
            pe.replay(g)

        @block.vector
        def _(g):
            dve.replay(g)

        @block.gpsimd
        def _(g):
            pool.replay(g)
    ctx.close()


def kernel(x, ctx_1024, g_xattn, g_ffn, L0_xattn_Wq, L0_xattn_bq, L0_xattn_Wk, L0_xattn_bk, L0_ffn_gate_w,
           L0_ffn_w_gate, L0_ffn_w_up, L0_ffn_w_down, L0_ffn_sh_gate, L0_ffn_sh_up, L0_ffn_sh_down):
    import numpy as np
    import concourse.bacc as bacc
    from concourse import mybir as mb
    from concourse.bass_utils import run_bass_kernel_spmd

    nc = bacc.Bacc("TRN2", target_bir_lowering=False, num_devices=1)
    cst = np.zeros((P, 2 * P + E + NT * ENTRY), np.float32)
    cst[:, 0:P] = np.eye(P, dtype=np.float32)
    cst[:, P:2 * P] = np.triu(np.ones((P, P), np.float32), 1)
    cst[:, 2 * P:2 * P + E] = 2 * SLOTS - CAP * np.arange(E)
    for t in range(NT):
        cst[:, 2 * P + E + t * ENTRY:2 * P + E + (t + 1) * ENTRY] = (P * t + np.arange(P))[:, None]
    tab0 = np.zeros((SLOTS, ENTRY), np.float32)
    tab0[:, :] = (T + np.arange(SLOTS) % CAP)[:, None]
    c = np.ascontiguousarray
    arrays = {
        "x": c(x), "ctxt": c(np.transpose(np.asarray(ctx_1024), (0, 2, 1))),
        "gx": c(np.asarray(g_xattn).reshape(1, 1)), "gf": c(np.asarray(g_ffn).reshape(1, 1)),
        "wq": c(np.asarray(L0_xattn_Wq).T), "bq": c(np.asarray(L0_xattn_bq).reshape(D, 1)),
        "wk": c(np.asarray(L0_xattn_Wk).T), "bk": c(np.asarray(L0_xattn_bk).reshape(D, 1)),
        "gw": c(np.asarray(L0_ffn_gate_w).T), "wg": c(L0_ffn_w_gate), "wu": c(L0_ffn_w_up), "wd": c(L0_ffn_w_down),
        "sg": c(np.asarray(L0_ffn_sh_gate).T), "su": c(np.asarray(L0_ffn_sh_up).T),
        "sd": c(np.asarray(L0_ffn_sh_down).T), "cst": cst,
        "tab0": tab0,
    }
    args = [nc.dram_tensor(f"i_{n}", a.shape, mb.dt.from_np(a.dtype), kind="ExternalInput").ap()
            for n, a in arrays.items()]
    y = nc.dram_tensor("o_y", (ROWS, H), FP, kind="ExternalOutput").ap()
    rows = nc.dram_tensor("rows", (ROWS, ROW), FP, kind="Internal").ap()
    table = nc.dram_tensor("table", (SLOTS, ENTRY), FP, kind="Internal").ap()
    build(nc, *args, y, rows, table)
    r = run_bass_kernel_spmd(nc, [{f"i_{n}": a for n, a in arrays.items()}], core_ids=[0])
    return r.results[0]["o_y"][0:T].reshape(B, L, H)
```
